# Optimizing a Trainium2 kernel written in Bass

```python
import numpy as np
import jax
import jax.numpy as jnp

def _softmax(x, axis=-1):
    return jax.nn.softmax(x, axis=axis)

def _gelu(x):
    return jax.nn.gelu(x, approximate=True)

def _silu(x):
    return jax.nn.silu(x)

def _sigmoid(x):
    return jax.nn.sigmoid(x)

def _layernorm(x, axis=-1, eps=1e-05):
    m = jnp.mean(x, axis=axis, keepdims=True)
    v = jnp.var(x, axis=axis, keepdims=True)
    return (x - m) / jnp.sqrt(v + eps)

def _scatter_add(tgt, idx, src, axis=0):
    return tgt.at[idx].add(src)

def _segment_sum(src, seg, n):
    return jax.ops.segment_sum(src, seg, n)
kernel_name = 'mk_cond_seq_d4_seqx_r8_fd9f0c'

def setup_inputs(seed: int=0):
    np.random.seed(seed)
    _w = jnp.asarray

    def _rec_inputs():
        import jax
        import jax.numpy as jnp
        _rk = jax.random.key(seed)
        x = -7.109e-05 + 0.9999 * jax.random.normal(jax.random.fold_in(_rk, 1), (32, 32, 128), jnp.float32)
        _lenS = 32 - jax.random.randint(jax.random.fold_in(_rk, 7), (32,), 0, max(1, 32 // 4) + 1, jnp.int32)
        _lenS2 = 32 - jax.random.randint(jax.random.fold_in(_rk, 8), (32,), 0, max(1, 32 // 4) + 1, jnp.int32)
        condB_theta = jax.random.uniform(jax.random.fold_in(_rk, 11), (32,), jnp.float32, 0.0, 0.983423)
        condB_phi = jax.random.uniform(jax.random.fold_in(_rk, 12), (32,), jnp.float32, 0.0, 0.961312)
        itok_B_34_63 = jax.random.randint(jax.random.fold_in(_rk, 14), (32,), 34, 64, jnp.int32)
        fside_Bx16xSxS_0 = -1.47943e-05 + 1.00017 * jax.random.normal(jax.random.fold_in(_rk, 15), (32, 16, 32, 32), jnp.float32)
        itok_B_0_15 = jax.random.randint(jax.random.fold_in(_rk, 16), (32,), 0, 16, jnp.int32)
        condB_gatescore = jax.random.uniform(jax.random.fold_in(_rk, 17), (32,), jnp.float32, 0.0, 0.581427)
        _validS = jnp.arange(32)[None, :] < _lenS[:, None]
        _validS2 = jnp.arange(32)[None, :] < _lenS2[:, None]
        _causal = jnp.tril(jnp.ones((32, 32), dtype=bool))
        mask_Bx1xSxS_bk0 = jnp.logical_not(jnp.broadcast_to(_validS[:, None, None, :], (32, 1, 32, 32)))
        return (x, condB_theta, condB_phi, itok_B_34_63, fside_Bx16xSxS_0, itok_B_0_15, condB_gatescore, mask_Bx1xSxS_bk0)
    x, condB_theta, condB_phi, itok_B_34_63, fside_Bx16xSxS_0, itok_B_0_15, condB_gatescore, mask_Bx1xSxS_bk0 = _rec_inputs()

    def _L0_cond_setup():
        import jax, jax.numpy as jnp
        import numpy as np
        key = jax.random.key(seed)
        k1, k2, k3 = jax.random.split(key, 3)
        B, N, D = (16, 512, 128)
        embeddings = jax.random.normal(k1, (B, N, D), dtype=jnp.float32)
        theta = jax.random.uniform(k2, (B,), dtype=jnp.float32)
        phi = jax.random.uniform(k3, (B,), dtype=jnp.float32)
        return {'embeddings': embeddings, 'theta': theta, 'phi': phi}
    _L0_cond_all = _L0_cond_setup()
    _L0_cond_in = {k: v for k, v in _L0_cond_all.items() if k in ()}
    del _L0_cond_all

    def _L1_cond_setup():
        import jax, jax.numpy as jnp
        import numpy as np
        import math
        D_MODEL = 128
        N_HEAD = 16
        HEAD_DIM = D_MODEL // N_HEAD
        D_FF = 512
        NUM_STEPS = 100.0
        RESCALE = 4000.0
        EPS = 1e-05

        def _sin_emb(t):
            half = D_MODEL // 2
            x = t.astype(jnp.float32) / NUM_STEPS * RESCALE
            freqs = jnp.exp(jnp.arange(half, dtype=jnp.float32) * (-math.log(10000.0) / (half - 1)))
            e = x[:, None] * freqs[None, :]
            return jnp.concatenate([jnp.sin(e), jnp.cos(e)], axis=-1)

        def _ln(x):
            m = jnp.mean(x, axis=-1, keepdims=True)
            v = jnp.var(x, axis=-1, keepdims=True)
            return (x - m) / jnp.sqrt(v + EPS)

        def _gelu2(x):
            return x * jax.nn.sigmoid(1.702 * x)
        key = jax.random.key(seed)
        ks = jax.random.split(key, 24)
        B, S, D, F = (4, 64, D_MODEL, D_FF)
        std = 0.02
        inp = {'src': jax.random.normal(ks[0], (B, S, D), dtype=jnp.float32), 'src_mask': jax.random.randint(ks[1], (B, 1, S, S), 0, 2).astype(bool), 'timestep': jax.random.randint(ks[2], (B,), 0, 100, dtype=jnp.int32), 'attention_bias': jax.random.normal(ks[3], (B, N_HEAD, S, S), dtype=jnp.float32), 'W_ada': jax.random.normal(ks[4], (D, 2 * D), dtype=jnp.float32) * std, 'b_ada': jnp.zeros((2 * D,), dtype=jnp.float32), 'Wq': jax.random.normal(ks[5], (D, D), dtype=jnp.float32) * std, 'bq': jnp.zeros((D,), dtype=jnp.float32), 'Wk': jax.random.normal(ks[6], (D, D), dtype=jnp.float32) * std, 'bk': jnp.zeros((D,), dtype=jnp.float32), 'Wv': jax.random.normal(ks[7], (D, D), dtype=jnp.float32) * std, 'bv': jnp.zeros((D,), dtype=jnp.float32), 'Wo': jax.random.normal(ks[8], (D, D), dtype=jnp.float32) * std, 'bo': jnp.zeros((D,), dtype=jnp.float32), 'W1': jax.random.normal(ks[9], (D, F), dtype=jnp.float32) * std, 'b1': jnp.zeros((F,), dtype=jnp.float32), 'W2': jax.random.normal(ks[10], (F, D), dtype=jnp.float32) * std, 'b2': jnp.zeros((D,), dtype=jnp.float32), 'g2': jnp.ones((D,), dtype=jnp.float32), 'beta2': jnp.zeros((D,), dtype=jnp.float32)}
        return inp
    _L1_cond_all = _L1_cond_setup()
    _L1_cond_in = {k: v for k, v in _L1_cond_all.items() if k in ('W_ada', 'b_ada', 'Wq', 'bq', 'Wk', 'bk', 'Wv', 'bv', 'Wo', 'bo', 'W1', 'b1', 'W2', 'b2', 'g2', 'beta2')}
    del _L1_cond_all

    def _L2_cond_setup():
        import jax, jax.numpy as jnp
        import numpy as np
        B, S, D = (32, 128, 128)
        A = 32
        E = 16
        LN_EPS = 1e-05
        key = jax.random.key(seed)
        ks = jax.random.split(key, 10)
        s = lambda fan_in: 1.0 / np.sqrt(fan_in)
        return {'hidden_states': jax.random.normal(ks[0], (B, S, D), dtype=jnp.float32), 'domain_id': jax.random.randint(ks[1], (B,), 0, E, dtype=jnp.int64), 'down_W': jax.random.uniform(ks[2], (A, D), jnp.float32, -s(D), s(D)), 'down_b': jax.random.uniform(ks[3], (A,), jnp.float32, -s(D), s(D)), 'up_W': jax.random.uniform(ks[4], (D, A), jnp.float32, -s(A), s(A)), 'up_b': jax.random.uniform(ks[5], (D,), jnp.float32, -s(A), s(A)), 'expert_W': jax.random.uniform(ks[6], (E, A, A), jnp.float32, -s(A), s(A)), 'expert_b': jax.random.uniform(ks[7], (E, A), jnp.float32, -s(A), s(A)), 'domain_emb': jax.random.normal(ks[8], (E, A), dtype=jnp.float32), 'ln_gamma': jnp.ones((D,), jnp.float32), 'ln_beta': jnp.zeros((D,), jnp.float32)}
    _L2_cond_all = _L2_cond_setup()
    _L2_cond_in = {k: v for k, v in _L2_cond_all.items() if k in ('down_W', 'down_b', 'up_W', 'up_b', 'expert_W', 'expert_b', 'domain_emb', 'ln_gamma', 'ln_beta')}
    del _L2_cond_all

    def _L3_cond_setup():
        import jax, jax.numpy as jnp
        import numpy as np
        D_MODEL = 128
        N_HEADS = 16
        D_HEAD = D_MODEL // N_HEADS
        D_FF = 512
        EPS = 1e-05

        def layernorm(x, gamma, beta):
            mu = jnp.mean(x, axis=-1, keepdims=True)
            var = jnp.var(x, axis=-1, keepdims=True)
            return (x - mu) * jax.lax.rsqrt(var + EPS) * gamma + beta
        key = jax.random.key(seed)
        ks = jax.random.split(key, 16)
        B, T = (4, 256)
        s = 1.0 / np.sqrt(D_MODEL)
        sf = 1.0 / np.sqrt(D_FF)
        return {'x': jax.random.normal(ks[0], (B, T, D_MODEL), jnp.float32), 'gate_score': jax.random.uniform(ks[1], (B,), jnp.float32), 'Wq': jax.random.normal(ks[2], (D_MODEL, D_MODEL), jnp.float32) * s, 'bq': jnp.zeros((D_MODEL,), jnp.float32), 'Wk': jax.random.normal(ks[3], (D_MODEL, D_MODEL), jnp.float32) * s, 'bk': jnp.zeros((D_MODEL,), jnp.float32), 'Wv': jax.random.normal(ks[4], (D_MODEL, D_MODEL), jnp.float32) * s, 'bv': jnp.zeros((D_MODEL,), jnp.float32), 'Wo': jax.random.normal(ks[5], (D_MODEL, D_MODEL), jnp.float32) * s, 'bo': jnp.zeros((D_MODEL,), jnp.float32), 'W1': jax.random.normal(ks[6], (D_MODEL, D_FF), jnp.float32) * s, 'b1': jnp.zeros((D_FF,), jnp.float32), 'W2': jax.random.normal(ks[7], (D_FF, D_MODEL), jnp.float32) * sf, 'b2': jnp.zeros((D_MODEL,), jnp.float32), 'gamma1': jnp.ones((D_MODEL,), jnp.float32), 'beta1': jnp.zeros((D_MODEL,), jnp.float32), 'gamma2': jnp.ones((D_MODEL,), jnp.float32), 'beta2': jnp.zeros((D_MODEL,), jnp.float32)}
    _L3_cond_all = _L3_cond_setup()
    _L3_cond_in = {k: v for k, v in _L3_cond_all.items() if k in ('Wq', 'bq', 'Wk', 'bk', 'Wv', 'bv', 'Wo', 'bo', 'W1', 'b1', 'W2', 'b2', 'gamma1', 'beta1', 'gamma2', 'beta2')}
    del _L3_cond_all
    return {'x': x, 'condB_theta': condB_theta, 'condB_phi': condB_phi, 'itok_B_34_63': itok_B_34_63, 'fside_Bx16xSxS_0': fside_Bx16xSxS_0, 'itok_B_0_15': itok_B_0_15, 'condB_gatescore': condB_gatescore, 'mask_Bx1xSxS_bk0': mask_Bx1xSxS_bk0, 'L1_cond_W_ada': _L1_cond_in['W_ada'], 'L1_cond_b_ada': _L1_cond_in['b_ada'], 'L1_cond_Wq': _L1_cond_in['Wq'], 'L1_cond_bq': _L1_cond_in['bq'], 'L1_cond_Wk': _L1_cond_in['Wk'], 'L1_cond_bk': _L1_cond_in['bk'], 'L1_cond_Wv': _L1_cond_in['Wv'], 'L1_cond_bv': _L1_cond_in['bv'], 'L1_cond_Wo': _L1_cond_in['Wo'], 'L1_cond_bo': _L1_cond_in['bo'], 'L1_cond_W1': _L1_cond_in['W1'], 'L1_cond_b1': _L1_cond_in['b1'], 'L1_cond_W2': _L1_cond_in['W2'], 'L1_cond_b2': _L1_cond_in['b2'], 'L1_cond_g2': _L1_cond_in['g2'], 'L1_cond_beta2': _L1_cond_in['beta2'], 'L2_cond_down_W': _L2_cond_in['down_W'], 'L2_cond_down_b': _L2_cond_in['down_b'], 'L2_cond_up_W': _L2_cond_in['up_W'], 'L2_cond_up_b': _L2_cond_in['up_b'], 'L2_cond_expert_W': _L2_cond_in['expert_W'], 'L2_cond_expert_b': _L2_cond_in['expert_b'], 'L2_cond_domain_emb': _L2_cond_in['domain_emb'], 'L2_cond_ln_gamma': _L2_cond_in['ln_gamma'], 'L2_cond_ln_beta': _L2_cond_in['ln_beta'], 'L3_cond_Wq': _L3_cond_in['Wq'], 'L3_cond_bq': _L3_cond_in['bq'], 'L3_cond_Wk': _L3_cond_in['Wk'], 'L3_cond_bk': _L3_cond_in['bk'], 'L3_cond_Wv': _L3_cond_in['Wv'], 'L3_cond_bv': _L3_cond_in['bv'], 'L3_cond_Wo': _L3_cond_in['Wo'], 'L3_cond_bo': _L3_cond_in['bo'], 'L3_cond_W1': _L3_cond_in['W1'], 'L3_cond_b1': _L3_cond_in['b1'], 'L3_cond_W2': _L3_cond_in['W2'], 'L3_cond_b2': _L3_cond_in['b2'], 'L3_cond_gamma1': _L3_cond_in['gamma1'], 'L3_cond_beta1': _L3_cond_in['beta1'], 'L3_cond_gamma2': _L3_cond_in['gamma2'], 'L3_cond_beta2': _L3_cond_in['beta2']}

def reference(x, condB_theta, condB_phi, itok_B_34_63, fside_Bx16xSxS_0, itok_B_0_15, condB_gatescore, mask_Bx1xSxS_bk0, L1_cond_W_ada, L1_cond_b_ada, L1_cond_Wq, L1_cond_bq, L1_cond_Wk, L1_cond_bk, L1_cond_Wv, L1_cond_bv, L1_cond_Wo, L1_cond_bo, L1_cond_W1, L1_cond_b1, L1_cond_W2, L1_cond_b2, L1_cond_g2, L1_cond_beta2, L2_cond_down_W, L2_cond_down_b, L2_cond_up_W, L2_cond_up_b, L2_cond_expert_W, L2_cond_expert_b, L2_cond_domain_emb, L2_cond_ln_gamma, L2_cond_ln_beta, L3_cond_Wq, L3_cond_bq, L3_cond_Wk, L3_cond_bk, L3_cond_Wv, L3_cond_bv, L3_cond_Wo, L3_cond_bo, L3_cond_W1, L3_cond_b1, L3_cond_W2, L3_cond_b2, L3_cond_gamma1, L3_cond_beta1, L3_cond_gamma2, L3_cond_beta2):
    import jax
    import jax.numpy as jnp

    def _L0_cond_ref(embeddings, theta, phi):
        import jax, jax.numpy as jnp
        import numpy as np
        B, N, D = embeddings.shape
        e = embeddings.reshape(B, N, D // 4, 4)
        ct = jnp.cos(theta)[:, None, None]
        st = jnp.sin(theta)[:, None, None]
        cp = jnp.cos(phi)[:, None, None]
        sp = jnp.sin(phi)[:, None, None]
        x0, x1, x2, x3 = (e[..., 0], e[..., 1], e[..., 2], e[..., 3])
        out = jnp.stack([x0 * ct + x1 * st, -x0 * st + x1 * ct, x2 * cp + x3 * sp, -x2 * sp + x3 * cp], axis=-1)
        return out.reshape(B, N, D)

    def _L1_cond_ref(src, src_mask, timestep, attention_bias, W_ada, b_ada, Wq, bq, Wk, bk, Wv, bv, Wo, bo, W1, b1, W2, b2, g2, beta2):
        import jax, jax.numpy as jnp
        import numpy as np
        import math
        D_MODEL = 128
        N_HEAD = 16
        HEAD_DIM = D_MODEL // N_HEAD
        D_FF = 512
        NUM_STEPS = 100.0
        RESCALE = 4000.0
        EPS = 1e-05

        def _sin_emb(t):
            half = D_MODEL // 2
            x = t.astype(jnp.float32) / NUM_STEPS * RESCALE
            freqs = jnp.exp(jnp.arange(half, dtype=jnp.float32) * (-math.log(10000.0) / (half - 1)))
            e = x[:, None] * freqs[None, :]
            return jnp.concatenate([jnp.sin(e), jnp.cos(e)], axis=-1)

        def _ln(x):
            m = jnp.mean(x, axis=-1, keepdims=True)
            v = jnp.var(x, axis=-1, keepdims=True)
            return (x - m) / jnp.sqrt(v + EPS)

        def _gelu2(x):
            return x * jax.nn.sigmoid(1.702 * x)
        B, S, D = src.shape
        emb = jax.nn.silu(_sin_emb(timestep)) @ W_ada + b_ada
        scale, shift = jnp.split(emb[:, None, :], 2, axis=-1)
        x = _ln(src) * (1.0 + scale) + shift
        q = (x @ Wq + bq).reshape(B, S, N_HEAD, HEAD_DIM).transpose(0, 2, 1, 3)
        k = (x @ Wk + bk).reshape(B, S, N_HEAD, HEAD_DIM).transpose(0, 2, 1, 3)
        v = (x @ Wv + bv).reshape(B, S, N_HEAD, HEAD_DIM).transpose(0, 2, 1, 3)
        scores = jnp.einsum('bhqd,bhkd->bhqk', q / math.sqrt(HEAD_DIM), k)
        scores = scores + attention_bias
        scores = jnp.where(src_mask, -jnp.inf, scores.astype(jnp.float32))
        probs = jax.nn.softmax(scores, axis=-1).astype(v.dtype)
        ctx = jnp.einsum('bhqk,bhkd->bhqd', probs, v)
        ctx = ctx.transpose(0, 2, 1, 3).reshape(B, S, D)
        x = x + (ctx @ Wo + bo)
        h = _ln(x) * g2 + beta2
        ff = _gelu2(h @ W1 + b1) @ W2 + b2
        return x + ff

    def _L2_cond_ref(hidden_states, domain_id, down_W, down_b, up_W, up_b, expert_W, expert_b, domain_emb, ln_gamma, ln_beta):
        import jax, jax.numpy as jnp
        import numpy as np
        B, S, D = (32, 128, 128)
        A = 32
        E = 16
        LN_EPS = 1e-05
        residual = hidden_states
        hidden = jnp.einsum('bsd,ad->bsa', hidden_states, down_W) + down_b
        hidden = jax.nn.gelu(hidden, approximate=False)
        valid = (domain_id >= 0) & (domain_id < E)
        idx = jnp.clip(domain_id, 0, E - 1)
        Wsel = expert_W[idx]
        bsel = expert_b[idx]
        expert_out = jnp.einsum('bsa,boa->bso', hidden, Wsel) + bsel[:, None, :]
        domain_output = jnp.where(valid[:, None, None], expert_out, hidden)
        hidden = domain_output + domain_emb[idx][:, None, :]
        hidden = jnp.einsum('bsa,da->bsd', hidden, up_W) + up_b
        x = hidden + residual
        mu = jnp.mean(x, axis=-1, keepdims=True)
        var = jnp.mean(jnp.square(x - mu), axis=-1, keepdims=True)
        return (x - mu) * jax.lax.rsqrt(var + LN_EPS) * ln_gamma + ln_beta

    def _L3_cond_ref(x, gate_score, Wq, bq, Wk, bk, Wv, bv, Wo, bo, W1, b1, W2, b2, gamma1, beta1, gamma2, beta2):
        import jax, jax.numpy as jnp
        import numpy as np
        D_MODEL = 128
        N_HEADS = 16
        D_HEAD = D_MODEL // N_HEADS
        D_FF = 512
        EPS = 1e-05

        def layernorm(x, gamma, beta):
            mu = jnp.mean(x, axis=-1, keepdims=True)
            var = jnp.var(x, axis=-1, keepdims=True)
            return (x - mu) * jax.lax.rsqrt(var + EPS) * gamma + beta
        B, T, C = x.shape
        h = layernorm(x, gamma1, beta1)
        Q = (h @ Wq + bq).reshape(B, T, N_HEADS, D_HEAD).transpose(0, 2, 1, 3)
        K = (h @ Wk + bk).reshape(B, T, N_HEADS, D_HEAD).transpose(0, 2, 1, 3)
        V = (h @ Wv + bv).reshape(B, T, N_HEADS, D_HEAD).transpose(0, 2, 1, 3)
        scores = jnp.einsum('bhqd,bhkd->bhqk', Q, K) / np.sqrt(D_HEAD)
        causal = jnp.tril(jnp.ones((T, T), dtype=bool))
        scores = jnp.where(causal, scores, -jnp.inf)
        attn = jax.nn.softmax(scores, axis=-1)
        ctx = jnp.einsum('bhqk,bhkd->bhqd', attn, V)
        ctx = ctx.transpose(0, 2, 1, 3).reshape(B, T, C)
        attn_out = ctx @ Wo + bo
        x1 = x + attn_out
        h2 = layernorm(x1, gamma2, beta2)
        ff = jax.nn.gelu(h2 @ W1 + b1, approximate=False) @ W2 + b2
        x2 = x1 + ff
        g = gate_score[:, None, None]
        return x + g * (x2 - x)
    x = _L0_cond_ref(x, condB_theta, condB_phi)
    x = _L1_cond_ref(x, mask_Bx1xSxS_bk0, itok_B_34_63, fside_Bx16xSxS_0, L1_cond_W_ada, L1_cond_b_ada, L1_cond_Wq, L1_cond_bq, L1_cond_Wk, L1_cond_bk, L1_cond_Wv, L1_cond_bv, L1_cond_Wo, L1_cond_bo, L1_cond_W1, L1_cond_b1, L1_cond_W2, L1_cond_b2, L1_cond_g2, L1_cond_beta2)
    x = _L2_cond_ref(x, itok_B_0_15, L2_cond_down_W, L2_cond_down_b, L2_cond_up_W, L2_cond_up_b, L2_cond_expert_W, L2_cond_expert_b, L2_cond_domain_emb, L2_cond_ln_gamma, L2_cond_ln_beta)
    x = _L3_cond_ref(x, condB_gatescore, L3_cond_Wq, L3_cond_bq, L3_cond_Wk, L3_cond_bk, L3_cond_Wv, L3_cond_bv, L3_cond_Wo, L3_cond_bo, L3_cond_W1, L3_cond_b1, L3_cond_W2, L3_cond_b2, L3_cond_gamma1, L3_cond_beta1, L3_cond_gamma2, L3_cond_beta2)
    return x

_drawn_inputs = setup_inputs


def setup_inputs(seed=0):
    import zlib

    import numpy as np

    out = dict(_drawn_inputs(seed))
    spreads = {'L1_cond_b_ada': (0.0, 0.1),
     'L1_cond_bq': (0.0, 0.8),
     'L1_cond_bk': (0.0, 0.8),
     'L1_cond_bv': (0.0, 0.398),
     'L1_cond_bo': (0.0, 0.1),
     'L1_cond_b1': (0.0, 0.427),
     'L1_cond_b2': (0.0, 0.1),
     'L1_cond_g2': (1.0, 0.6),
     'L1_cond_beta2': (0.0, 0.8),
     'L2_cond_ln_gamma': (1.0, 0.2),
     'L2_cond_ln_beta': (0.0, 0.1),
     'L3_cond_bq': (0.0, 0.797),
     'L3_cond_bk': (0.0, 0.8),
     'L3_cond_bv': (0.0, 0.1),
     'L3_cond_bo': (0.0, 0.1),
     'L3_cond_b1': (0.0, 0.378),
     'L3_cond_b2': (0.0, 0.1),
     'L3_cond_gamma1': (1.0, 0.2),
     'L3_cond_beta1': (0.0, 0.1),
     'L3_cond_gamma2': (1.0, 0.2),
     'L3_cond_beta2': (0.0, 0.356)}
    factors = {'fside_Bx16xSxS_0': 6.019,
     'L1_cond_Wq': 8.0,
     'L1_cond_Wk': 8.0,
     'L1_cond_Wv': 4.078,
     'L2_cond_down_b': 5.717}
    for name, (base, spread) in spreads.items():
        noise = np.random.default_rng([zlib.crc32(name.encode()), seed]).standard_normal(out[name].shape)
        drawn = base * np.exp(spread * noise) if base else spread * noise
        out[name] = jnp.asarray(drawn.astype(out[name].dtype))
    for name, factor in factors.items():
        out[name] = (out[name] * factor).astype(out[name].dtype)
    return out
```

```python
from contextlib import ExitStack

import numpy as np

import concourse.bass as bass
from concourse import mybir

F32 = mybir.dt.float32
I32 = mybir.dt.int32
U8 = mybir.dt.uint8
ALU = mybir.AluOpType
ACT = mybir.ActivationFunctionType
AX = mybir.AxisListType

B, S, D, F, H = 32, 32, 128, 512, 16
DH = D // H
P = 128
HALVES = 2
HB = B // HALVES
TOK = HB * S
TILES = TOK // P
TB = P // S
G = D // 32
J = 32 // DH
FC = F // P
A, E = 32, 16
EPS = 1e-5
MASKED = -1e30
MAGIC = 12582912.0
TWO_PI_HI = 6.28125
TWO_PI_LO = 2 * np.pi - TWO_PI_HI
PI_BELOW = 3.1415925
NSTAT = 6

COLS = {}
for _name, _width in [("bq1", 1), ("bk1", 1), ("bv1", 1), ("g1", 1), ("beta1", 1), ("b11", FC),
                      ("bq3", 1), ("bk3", 1), ("bv3", 1), ("gin3", 1), ("bin3", 1), ("g3", 1),
                      ("beta3", 1), ("b13", FC), ("down_b", 1), ("down_wT", A)]:
    _at = sum(w for _, w in COLS.values())
    COLS[_name] = (_at, _width)
NCOLS = sum(w for _, w in COLS.values())

ROWS = ["ada_scale", "ada_shift", "bo1", "b21", "up_b", "ln_g", "ln_b", "bo3", "b23"]

CONSTS = {}
for _name, _width in [("ident", P), ("qspread", J), ("kspread", G), ("ones_diag", 32), ("causal", S),
                      ("freq", 1), ("turns", 1), ("phase", 1), ("to_tokens", P), ("expert_no", 1),
                      ("row_e", 1)]:
    _at = sum(w for _, w in CONSTS.values())
    CONSTS[_name] = (_at, _width)
NCONSTS = sum(w for _, w in CONSTS.values())


def shape_constants():
    c = np.zeros((P, NCONSTS), np.float32)
    p = np.arange(P)

    def put(name, value):
        at, width = CONSTS[name]
        c[:, at:at + width] = value

    put("ident", np.eye(P))
    put("qspread", (p[:, None] % 32 // DH == np.arange(J)) * DH ** -0.5)
    put("kspread", p[:, None] // 32 == np.arange(G))
    put("ones_diag", p[:, None] // S == np.arange(32) // DH)
    put("causal", np.where(np.arange(S) <= p[:, None] % S, 0.0, MASKED))
    half = D // 2
    freqs = np.exp(np.arange(half, dtype=np.float32) * np.float32(-np.log(10000.0) / (half - 1)))
    put("freq", np.concatenate([freqs, freqs])[:, None])
    put("turns", np.where(p < half, 0.0, 0.25)[:, None])
    put("phase", np.where(p < half, 0.0, np.pi / 2)[:, None])
    put("to_tokens", np.where(p[:, None] < TB, p[:, None] == p // S, 0))
    put("expert_no", p[:, None])
    put("row_e", p[:, None] == E)
    return c


def cond_seq(nc, x, fside, mask, cols, rows, consts, w_ada, w1, w3, experts, up_wT, scalars, steps,
             domains, out):
    with ExitStack() as ctx:
        def sb(name, shape, dt=F32):
            return ctx.enter_context(nc.sbuf_tensor(name, shape, dt))

        def sem(name):
            return ctx.enter_context(nc.semaphore(name))

        cols_sb = sb("cols_sb", [P, NCOLS])
        rows_sb = sb("rows_sb", [P, len(ROWS), D])
        const_sb = sb("const_sb", [P, NCONSTS])
        wada_sb = sb("wada_sb", [P, 2 * D])
        w_sb = {1: sb("w1_sb", [P, 4 * D + 2 * F]), 3: sb("w3_sb", [P, 4 * D + 2 * F])}
        expert_sb = sb("expert_sb", [E + 1, A * A + 2 * A])
        up_sb = sb("up_sb", [A, D])
        scalar_sb = sb("scalar_sb", [TB, 3, HALVES * TILES])
        steps_sb = sb("steps_sb", [P, B], I32)
        domain_sb = sb("domain_sb", [E + 1, B], I32)

        def col(name):
            at, width = COLS[name]
            return cols_sb[:, at:at + width]

        def row(name):
            return rows_sb[:, ROWS.index(name), :]

        def const(name, rows_=P):
            at, width = CONSTS[name]
            return const_sb[0:rows_, at:at + width]

        ident = const("ident")
        wq, wk, wv, wo, wf1, wf2 = ({} for _ in range(6))
        for layer in (1, 3):
            w = w_sb[layer]
            wq[layer], wk[layer], wv[layer], wo[layer] = (w[:, i * D:(i + 1) * D] for i in range(4))
            wf1[layer] = w[:, 4 * D:4 * D + F]
            wf2[layer] = w[:, 4 * D + F:4 * D + 2 * F].rearrange("p (c n) -> p c n", c=FC)

        angle = sb("angle", [TB, HALVES * TILES, 8])
        turn = sb("turn", [TB, HALVES * TILES, 8])
        rot4 = sb("rot4", [TB, HALVES * TILES, 9])
        rot = sb("rot", [P, HALVES * TILES, 9])
        emb_e = sb("emb_e", [P, B])
        emb_t = sb("emb_t", [P, B])
        emb_s = sb("emb_s", [P, B])
        emb_tok = sb("emb_tok", [P, B, S])
        hot = sb("hot", [E + 1, 6, B])
        wselT = sb("wselT", [A, B, A])
        ebias = sb("ebias", [A, B])
        qbias = sb("qbias", [P, 2, J])
        bo_all = sb("bo_all", [P, 2, D])
        half_pow = sb("half_pow", [P, TILES])

        def each(name, shape, dt=F32):
            return [sb(f"{name}_{h}", shape, dt) for h in range(HALVES)]

        xin = each("xin", [P, TILES, D])
        xrot = each("xrot", [P, TILES, D])
        res = each("res", [P, TILES, D])
        res_b = each("res_b", [P, TILES, D])
        mid = each("mid", [P, TILES, D])
        mid_b = each("mid_b", [P, TILES, D])
        post = each("post", [P, TILES, D])
        post_b = each("post_b", [P, TILES, D])
        norm = each("norm", [P, TILES, D])
        ada = each("ada", [P, TILES, 2 * D])
        stats = each("stats", [P, TILES, NSTAT])
        mv = each("mv", [P, TILES, 2])
        rstd = each("rstd", [P, TILES])
        feat = each("feat", [P, TOK])
        qs = each("qs", [P, HB, J, S])
        ks = each("ks", [P, HB, G, S])
        vs = each("vs", [P, HB, G, 32])
        bias = each("bias", [P, HB, G, S])
        mask_u8 = each("mask_u8", [P, HB, S], U8)
        mask_f = each("mask_f", [P, HB, S])
        sc = each("sc", [P, HB, G, S])
        peak = each("peak", [P, HB, G])
        pt = each("pt", [P, HB, G, S])
        rsum = each("rsum", [P, TOK])
        ctxT = each("ctxT", [P, TOK])
        act = [q[:, :, :, :].rearrange("p b j s -> p (b j s)").rearrange("p (c n) -> p c n", c=FC) for q in qs]
        hid = [c[0:A, :] for c in ctxT]
        hid2 = [r[0:A, :] for r in rsum]

        ps = [ctx.enter_context(nc.psum_tensor(f"ps_{h}", [P, 4, 512], F32)) for h in range(HALVES)]

        def tiles(h, bank):
            return ps[h][:, bank, :].rearrange("p (t n) -> p t n", t=TILES)

        consts_in, cols_in, rows_in, wada_in = (sem(n) for n in ("consts_in", "cols_in", "rows_in", "wada_in"))
        w_in = {1: sem("w1_in"), 3: sem("w3_in")}
        small_in, up_in, expert_in = sem("small_in"), sem("up_in"), sem("expert_in")
        x_in = [sem(f"x_in_{h}") for h in range(HALVES)]
        bias_in = [sem(f"bias_in_{h}") for h in range(HALVES)]
        mask_in = [sem(f"mask_in_{h}") for h in range(HALVES)]
        out_done = sem("out_done")

        (vs_zeroed, pow_set, angles_set, sin_set, rot_spread, rot_set, emb_angle, emb_sin, emb_exp, emb_set,
         dve_setup, hot_set, sel_made, sel_set, ebias_made, bo_made, bo_set, qbias_set) = (
            sem(n) for n in ("vs_zeroed", "pow_set", "angles_set", "sin_set", "rot_spread", "rot_set",
                             "emb_angle", "emb_sin", "emb_exp", "emb_set", "dve_setup", "hot_set",
                             "sel_made", "sel_set", "ebias_made", "bo_made", "bo_set", "qbias_set"))

        def per_half(name):
            return [sem(f"{name}_{h}") for h in range(HALVES)]

        bias_masked, mask_scaled = per_half("bias_masked"), per_half("mask_scaled")
        rotated, ada_made, ada_set, modulated = (per_half(n) for n in ("rotated", "ada_made", "ada_set", "modulated"))
        x2_T, x2_copied, down_made, down_act = (per_half(n) for n in ("x2_T", "x2_copied", "down_made", "down_act"))
        expert_made, expert_biased, up_made = (per_half(n) for n in ("expert_made", "expert_biased", "up_made"))
        adapted, res3_set, gated = (per_half(n) for n in ("adapted", "res3_set", "gated"))

        stats_made, stats_summed, scale_made, normed = (
            per_half(n) for n in ("stats_made", "stats_summed", "scale_made", "normed"))

        def upto_norm(n, count, each_norm):
            return n * each_norm + count

        def upto(layer, count, each_layer):
            return (layer // 2) * each_layer + count

        (in_T, feat_ready, q_made, k_made, q_spread, k_spread, v_made, v_spread, scored,
         biased, peaked, shifted, exped, prob_T, ctx_made, sum_made, recip_made, ctx_ready, attn_made,
         mid_ready, res_b_ready, mid_b_ready, mid_T, mid_feat, ffn1_made, ffn_act, ffn2_made, post_ready) = (
            per_half(n) for n in ("in_T", "feat_ready", "q_made", "k_made", "q_spread", "k_spread",
                                   "v_made", "v_spread", "scored", "biased", "peaked",
                                   "shifted", "exped", "prob_T", "ctx_made", "sum_made", "recip_made",
                                   "ctx_ready", "attn_made", "mid_ready", "res_b_ready", "mid_b_ready",
                                   "mid_T", "mid_feat", "ffn1_made", "ffn_act", "ffn2_made", "post_ready"))

        PAIRS = (0, 1)

        def pair(tensor, h, n):
            return tensor[h][:, 8 * n:8 * n + 8]

        block = ctx.enter_context(nc.Block())

        @block.sync
        def _(sp):
            sp.dma_start(scalar_sb[:, :, :], scalars).then_inc(small_in, 16)
            sp.dma_start(const_sb[:, :], consts).then_inc(consts_in, 16)
            sp.dma_start(steps_sb[:, :], steps.partition_broadcast(P)).then_inc(small_in, 16)
            sp.dma_start(xin[0][:, :, :], x[:, 0:TILES, :]).then_inc(x_in[0], 16)
            sp.dma_start(w_sb[1][:, :], w1).then_inc(w_in[1], 16)
            for h in range(HALVES):
                sp.dma_start(bias[h][:, :, :, :], fside[:, h * HB:(h + 1) * HB]).then_inc(bias_in[h], 16)
            sp.dma_start(w_sb[3][:, :], w3).then_inc(w_in[3], 16)
            for h in range(HALVES):
                sp.wait_ge(gated[h], TILES)
                dst = out.rearrange("(u b) s d -> (b s) u d", b=TB)[:, h * TILES:(h + 1) * TILES, :]
                sp.dma_start(dst, post[h][:, :, :]).then_inc(out_done, 16)
            sp.wait_ge(out_done, 16 * HALVES)

        @block.gpsimd
        def _(pool):
            pool.memset(half_pow[:, :], -0.5).then_inc(pow_set, 1)
            for h in range(HALVES):
                pool.memset(vs[h][:, :, :, :], 0.0).then_inc(vs_zeroed, 1)
            for h in range(HALVES):
                pool.wait_ge(mask_in[h], 16 * J)
                pool.tensor_scalar(mask_f[h][:, :, :], mask_u8[h][:, :, :], MASKED, None,
                                   ALU.mult).then_inc(mask_scaled[h], 1)

            def norm_scale(n, h):
                pool.wait_ge(stats_summed[h], upto_norm(n, TILES + 1, TILES + 1))
                pool.tensor_tensor(rstd[h][:, :], rstd[h][:, :], half_pow[:, :],
                                   ALU.pow).then_inc(scale_made[h], 1)

            def mask_bias(h):
                pool.wait_ge(bias_in[h], 16)
                pool.wait_ge(mask_scaled[h], 1)
                for i in range(4):
                    part = bias[h][:, 4 * i:4 * i + 4]
                    pool.tensor_tensor(part, part,
                                       mask_f[h][:, 4 * i:4 * i + 4, :].unsqueeze(2).to_broadcast([P, 4, G, S]),
                                       ALU.add).then_inc(bias_masked[h], 1)

            def add_row(dst, src, what):
                return pool.tensor_tensor(dst, src, what.unsqueeze(1).to_broadcast([P, TILES, D]), ALU.add)

            def residual_in(layer, h):
                pool.wait_ge(bo_set, layer // 2 + 1)
                pool.wait_ge(modulated[h] if layer == 1 else res3_set[h], 2)
                add_row(res_b[h][:, :, :], res[h][:, :, :], bo_all[:, layer // 2, :]).then_inc(res_b_ready[h], 1)

            def residual_mid(layer, h):
                pool.wait_ge(mid_ready[h], upto(layer, 1, 1))
                add_row(mid_b[h][:, :, :], mid[h][:, :, :], row("b21" if layer == 1 else "b23"))\
                    .then_inc(mid_b_ready[h], 1)
                if layer == 3:
                    pool.wait_ge(mid_b_ready[h], upto(3, 1, 1))
                    pool.tensor_tensor(mid_b[h][:, :, :], mid_b[h][:, :, :], res[h][:, :, :],
                                       ALU.subtract).then_inc(mid_b_ready[h], 1)

            pool.wait_ge(pow_set, 1)
            pool.wait_ge(rows_in, 16)
            norm_scale(0, 0)
            norm_scale(0, 1)
            mask_bias(0)
            residual_in(1, 0)
            mask_bias(1)
            residual_in(1, 1)
            for h in range(HALVES):
                norm_scale(1, h)
                residual_mid(1, h)
            for h in range(HALVES):
                pool.wait_ge(post_ready[h], 1)
                add_row(post_b[h][:, :, :], post[h][:, :, :], row("up_b")).then_inc(post_ready[h], 1)
            for h in range(HALVES):
                norm_scale(2, h)
                norm_scale(3, h)
                residual_in(3, h)
            for h in range(HALVES):
                norm_scale(4, h)
                residual_mid(3, h)

        def v_copy(copy, h, j):
            src = ps[h][j * 32:(j + 1) * 32, 2, :].rearrange("p (n d) -> p n d", d=DH)
            dst = vs[h][j * 32:(j + 1) * 32].rearrange("p b g f -> p (b g) f")
            return copy(dst[:, :, j * DH:(j + 1) * DH], src)

        @block.scalar
        def _(sca):
            sca.dma_start(xin[1][:, :, :], x[:, TILES:2 * TILES, :]).then_inc(x_in[1], 16)
            sca.dma_start(wada_sb[:, :], w_ada).then_inc(wada_in, 16)
            sca.dma_start(rows_sb[:, :, :], rows.partition_broadcast(P)).then_inc(rows_in, 16)
            sca.dma_start(cols_sb[:, :], cols).then_inc(cols_in, 16)
            for h in range(HALVES):
                for j in range(J):
                    sca.dma_start(mask_u8[h][j * S:(j + 1) * S, :, :],
                                  mask[:, h * HB:(h + 1) * HB, :]).then_inc(mask_in[h], 16)
            sca.dma_start(domain_sb[:, :], domains.partition_broadcast(E + 1)).then_inc(expert_in, 16)
            sca.dma_start(expert_sb[0:E, :], experts).then_inc(expert_in, 16)
            at = CONSTS["ident"][0]
            sca.dma_start(expert_sb[E:E + 1, 0:A * A].rearrange("p (o a) -> p o a", o=A),
                          consts[0:A, at:at + A].unsqueeze(0)).then_inc(expert_in, 16)
            sca.dma_start(up_sb[:, :], up_wT).then_inc(up_in, 16)

            sca.wait_ge(angles_set, 1)
            sca.activation(rot4[:, :, 0:8], angle[:, :, :], ACT.Sin).then_inc(sin_set, 1)
            sca.wait_ge(emb_angle, 1)
            sca.activation(emb_s[:, :], emb_e[:, :], ACT.Sin).then_inc(emb_sin, 1)
            sca.wait_ge(emb_sin, 1)
            sca.activation(emb_t[:, :], emb_s[:, :], ACT.Exp, scale=-1.0).then_inc(emb_exp, 1)

            def features(layer, h):
                sca.wait_ge(in_T[h], upto(layer, 1, 1))
                if layer == 1:
                    sca.activation(feat[h][:, :], ps[h][:, 3, :], ACT.Copy).then_inc(feat_ready[h], 1)
                else:
                    sca.activation(feat[h][:, :], ps[h][:, 3, :], ACT.Identity, scale=col("gin3"),
                                   bias=col("bin3")).then_inc(feat_ready[h], 1)

            def spread_q(layer, h):
                sca.wait_ge(q_made[h], upto(layer, 1, 1))
                sca.wait_ge(qbias_set, 2)
                for j in range(J):
                    sca.activation(qs[h][:, :, j, :], ps[h][:, 0, :].rearrange("p (b s) -> p b s", b=HB),
                                   ACT.Identity, scale=const("qspread")[:, j:j + 1],
                                   bias=qbias[:, layer // 2, j:j + 1]).then_inc(q_spread[h], 1)

            def spread_v(layer, h):
                sca.wait_ge(v_made[h], upto(layer, 1, 1))
                sca.wait_ge(vs_zeroed, h + 1)
                for j in (0, 1):
                    v_copy(sca.copy, h, j).then_inc(v_spread[h], 1)

            def exps(layer, h):
                for n, pr in enumerate(PAIRS):
                    sca.wait_ge(shifted[h], upto(layer, n + 1, 2))
                    sca.activation(pair(sc, h, pr), pair(sc, h, pr), ACT.Exp).then_inc(exped[h], 1)

            def ffn_features(layer, h):
                sca.wait_ge(mid_T[h], upto(layer, 1, 1))
                sca.activation(feat[h][:, :], ps[h][:, 1, :], ACT.Identity, scale=col(f"g{layer}"),
                               bias=col(f"beta{layer}")).then_inc(mid_feat[h], 1)

            def ffn_gelu(layer, h):
                func = ACT.Gelu_apprx_sigmoid if layer == 1 else ACT.Gelu
                for c in range(FC):
                    sca.wait_ge(ffn1_made[h], upto(layer, c + 1, FC))
                    sca.activation(act[h][:, c, :], ps[h][:, c, :], func,
                                   bias=col(f"b1{layer}")[:, c:c + 1]).then_inc(ffn_act[h], 1)

            def adapter(h):
                sca.wait_ge(x2_T[h], 1)
                sca.activation(feat[h][:, :], ps[h][:, 1, :], ACT.Copy).then_inc(x2_copied[h], 1)

            def adapter_gelu(h):
                sca.wait_ge(down_made[h], 1)
                sca.activation(hid[h][:, :], ps[h][0:A, 2, :], ACT.Gelu,
                               bias=col("down_b")[0:A, :]).then_inc(down_act[h], 1)

            sca.wait_ge(cols_in, 16)
            for layer in (1, 3):
                for h in range(HALVES):
                    features(layer, h)
                    spread_q(layer, h)
                    spread_v(layer, h)
                for h in range(HALVES):
                    exps(layer, h)
                for h in range(HALVES):
                    ffn_features(layer, h)
                for h in range(HALVES):
                    ffn_gelu(layer, h)
                if layer == 1:
                    for h in range(HALVES):
                        adapter(h)
                        adapter_gelu(h)

        @block.tensor
        def _(pe):
            def transpose_tiles(src, h, bank):
                for t in range(TILES):
                    last = pe.transpose(ps[h][:, bank, t * P:(t + 1) * P], src[h][:, t, :], ident)
                return last

            pe.wait_ge(consts_in, 16)
            pe.wait_ge(sin_set, 1)
            pe.wait_ge(dve_setup, 1)
            pe.matmul(ps[0][:, 3, 0:HALVES * TILES * 9], const("to_tokens", TB),
                      rot4[:, :, :].rearrange("p t c -> p (t c)"), start=True, stop=True).then_inc(rot_spread, 1)
            pe.wait_ge(wada_in, 16)
            pe.wait_ge(emb_set, 1)

            def ada_product(h):
                for t in range(TILES):
                    b0 = h * HB + t * TB
                    last = pe.matmul(ps[h][:, t // 2, (t % 2) * 2 * D:(t % 2 + 1) * 2 * D],
                                     emb_tok[:, b0:b0 + TB, :].rearrange("p b s -> p (b s)"),
                                     wada_sb[:, :], start=True, stop=True)
                last.then_inc(ada_made[h], 1)

            ada_product(0)
            ada_product(1)

            pe.wait_ge(w_in[1], 16)
            pe.wait_ge(cols_in, 16)
            pe.matmul(ps[0][:, 2, 0:D], col("bv1").to_broadcast([P, P]), wo[1], start=True,
                      stop=True).then_inc(bo_made, 1)

            def expert_setup():
                pe.wait_ge(expert_in, 48)
                pe.wait_ge(hot_set, 6)
                for o in range(A):
                    last = pe.matmul(ps[1][0:A, 2 + o // 16, (o % 16) * B:(o % 16 + 1) * B],
                                     expert_sb[:, o * A:(o + 1) * A], hot[:, 5, :], start=True, stop=True)
                last.then_inc(sel_made, 1)
                pe.matmul(ps[0][0:A, 2, 256:256 + B], expert_sb[0:E, A * A:A * A + A], hot[0:E, 5, :],
                          start=True, stop=False)
                pe.matmul(ps[0][0:A, 2, 256:256 + B], expert_sb[0:E, A * A + A:A * A + 2 * A], hot[0:E, 1, :],
                          start=False, stop=True).then_inc(ebias_made, 1)

            def project(layer, h):
                if (layer, h) == (1, 0):
                    pe.wait_ge(ada_set[h], 1)
                pe.wait_ge(feat_ready[h], upto(layer, 1, 1))
                pe.matmul(ps[h][:, 0, :], wq[layer], feat[h][:, :], start=True, stop=True).then_inc(q_made[h], 1)
                pe.matmul(ps[h][:, 1, :], wk[layer], feat[h][:, :], start=True, stop=True).then_inc(k_made[h], 1)

            def values(layer, h):
                for b in range(HB):
                    for j in range(J):
                        last = pe.matmul(ps[h][j * 32:(j + 1) * 32, 2, b * 32:(b + 1) * 32],
                                         feat[h][:, b * S:(b + 1) * S],
                                         wv[layer].rearrange("p (g f) -> p g f", g=G)[:, :, j * DH:(j + 1) * DH],
                                         start=True, stop=True)
                last.then_inc(v_made[h], 1)

            def scores(layer, h):
                pe.wait_ge(q_spread[h], upto(layer, J, J))
                pe.wait_ge(k_spread[h], upto(layer, G, G))
                for pr in PAIRS:
                    if pr == 1:
                        pe.wait_ge(v_spread[h], upto(layer, J, J))
                    for i in range(8):
                        b = 8 * pr + i
                        last = pe.matmul(ps[h][:, 2 * pr + i // 4, (i % 4) * P:(i % 4 + 1) * P],
                                         qs[h][:, b].rearrange("p j s -> p (j s)"),
                                         ks[h][:, b].rearrange("p g s -> p (g s)"), start=True, stop=True)
                    last.then_inc(scored[h], 1)

            def context(layer, h):
                for n, pr in enumerate(PAIRS):
                    pe.wait_ge(prob_T[h], upto(layer, n + 1, 2))
                    for i in range(8):
                        b = 8 * pr + i
                        for g in range(G):
                            last = pe.matmul(ps[h][32 * g:32 * g + 32, 2, b * S:(b + 1) * S],
                                             vs[h][:, b, g, :], pt[h][:, b, g, :], start=True, stop=True)
                last.then_inc(ctx_made[h], 1)
                for g in range(G):
                    last = pe.matmul(ps[h][32 * g:32 * g + 32, 3, :], const("ones_diag"), pt[h][:, :, g, :],
                                     start=True, stop=True)
                last.then_inc(sum_made[h], 1)

            def attn_out(layer, h):
                pe.wait_ge(ctx_ready[h], upto(layer, 1, 1))
                for t in range(TILES):
                    last = pe.matmul(ps[h][:, 0, t * D:(t + 1) * D], ctxT[h][:, t * P:(t + 1) * P], wo[layer],
                                     start=True, stop=True)
                last.then_inc(attn_made[h], 1)

            def ffn_in(layer, h):
                pe.wait_ge(normed[h], upto_norm(1 if layer == 1 else 4, TILES, TILES))
                transpose_tiles(norm, h, 1).then_inc(mid_T[h], 1)

            def ffn(layer, h):
                pe.wait_ge(mid_feat[h], upto(layer, 1, 1))
                for c in range(FC):
                    pe.matmul(ps[h][:, c, :], wf1[layer][:, c * P:(c + 1) * P], feat[h][:, :], start=True,
                              stop=True).then_inc(ffn1_made[h], 1)

            def ffn_out(layer, h):
                pe.wait_ge(ffn_act[h], upto(layer, FC, FC))
                for t in range(TILES):
                    for c in range(FC):
                        last = pe.matmul(ps[h][:, 0, t * D:(t + 1) * D], act[h][:, c, t * P:(t + 1) * P],
                                         wf2[layer][:, c, :], start=(c == 0), stop=(c == FC - 1))
                last.then_inc(ffn2_made[h], 1)

            def adapter_down(h):
                pe.wait_ge(post_ready[h], 1)
                transpose_tiles(post, h, 1).then_inc(x2_T[h], 1)
                pe.wait_ge(x2_copied[h], 1)
                pe.matmul(ps[h][0:A, 2, :], col("down_wT"), feat[h][:, :], start=True, stop=True)\
                    .then_inc(down_made[h], 1)

            def adapter_expert(h):
                pe.wait_ge(down_act[h], 1)
                pe.wait_ge(sel_set, 1)
                for b in range(HB):
                    last = pe.matmul(ps[h][0:A, 3, b * S:(b + 1) * S], wselT[:, h * HB + b, :],
                                     hid[h][:, b * S:(b + 1) * S], start=True, stop=True)
                last.then_inc(expert_made[h], 1)

            def adapter_up(h):
                pe.wait_ge(expert_biased[h], 1)
                pe.wait_ge(up_in, 16)
                for t in range(TILES):
                    last = pe.matmul(ps[h][:, 0, t * D:(t + 1) * D], hid2[h][:, t * P:(t + 1) * P], up_sb[:, :],
                                     start=True, stop=True)
                last.then_inc(up_made[h], 1)

            for h in range(HALVES):
                pe.wait_ge(modulated[h], 2)
                if h == 0:
                    pe.wait_ge(rot_set, 1)
                transpose_tiles(res, h, 3).then_inc(in_T[h], 1)
            for layer in (1, 3):
                if layer == 3:
                    for h in range(HALVES):
                        pe.wait_ge(normed[h], upto_norm(3, TILES, TILES))
                        transpose_tiles(norm, h, 3).then_inc(in_T[h], 1)
                for h in range(HALVES):
                    project(layer, h)
                    if (layer, h) == (1, 0):
                        pe.wait_ge(bo_set, 1)
                    values(layer, h)
                    scores(layer, h)
                for h in range(HALVES):
                    context(layer, h)
                for h in range(HALVES):
                    attn_out(layer, h)
                for h in range(HALVES):
                    ffn_in(layer, h)
                if layer == 1:
                    pe.wait_ge(w_in[3], 16)
                    pe.matmul(ps[1][:, 2, 0:D], col("bv3").to_broadcast([P, P]), wo[3], start=True,
                              stop=True).then_inc(bo_made, 1)
                    pe.wait_ge(bo_set, 2)
                    expert_setup()
                    pe.wait_ge(sel_set, 1)
                    pe.wait_ge(dve_setup, 2)
                for h in range(HALVES):
                    ffn(layer, h)
                for h in range(HALVES):
                    ffn_out(layer, h)
                if layer == 1:
                    for h in range(HALVES):
                        adapter_down(h)
                    for h in range(HALVES):
                        adapter_expert(h)
                    for h in range(HALVES):
                        adapter_up(h)

        @block.vector
        def _(dve):
            NT = HALVES * TILES

            def reduce_angle(a, t, turns, phase, done):
                dve.tensor_scalar(t, a, 1 / (2 * np.pi), turns, ALU.mult, ALU.add).then_inc(done, 1)
                dve.wait_ge(done, 1)
                dve.tensor_scalar(t, t, MAGIC, None, ALU.add).then_inc(done, 1)
                dve.wait_ge(done, 2)
                dve.tensor_scalar(t, t, -MAGIC, None, ALU.add).then_inc(done, 1)
                dve.wait_ge(done, 3)
                dve.scalar_tensor_tensor(a, t, -TWO_PI_HI, a, ALU.mult, ALU.add).then_inc(done, 1)
                dve.wait_ge(done, 4)
                dve.scalar_tensor_tensor(a, t, -float(TWO_PI_LO), a, ALU.mult, ALU.add).then_inc(done, 1)
                dve.wait_ge(done, 5)
                dve.tensor_scalar(a, a, phase, PI_BELOW, ALU.add, ALU.min).then_inc(done, 1)
                dve.wait_ge(done, 6)
                return dve.tensor_scalar(a, a, -PI_BELOW, None, ALU.max)

            angle_parts = sem("angle_parts")
            cos_reduced, sin_reduced, emb_reduced = sem("cos_reduced"), sem("sin_reduced"), sem("emb_reduced")
            dve.wait_ge(small_in, 32)
            for which in range(2):
                src = scalar_sb[:, which, :]
                for c in (2 * which, 2 * which + 1, 4 + 2 * which):
                    dve.tensor_copy(angle[:, :, c], src).then_inc(angle_parts, 1)
                dve.tensor_scalar(angle[:, :, 5 + 2 * which], src, -1.0, None, ALU.mult).then_inc(angle_parts, 1)
            dve.tensor_copy(rot4[:, :, 8], scalar_sb[:, 2, :]).then_inc(dve_setup, 1)
            dve.wait_ge(angle_parts, 8)
            reduce_angle(angle[:, :, 0:4], turn[:, :, 0:4], 0.25, float(np.pi / 2), cos_reduced).then_inc(cos_reduced, 1)
            dve.wait_ge(cos_reduced, 7)
            reduce_angle(angle[:, :, 4:8], turn[:, :, 4:8], 0.0, 0.0, sin_reduced).then_inc(angles_set, 1)

            emb_step = sem("emb_step")
            dve.wait_ge(consts_in, 16)
            dve.tensor_copy(emb_t[:, :], steps_sb[:, :]).then_inc(emb_step, 1)
            dve.wait_ge(emb_step, 1)
            dve.tensor_scalar(emb_e[:, :], emb_t[:, :], 40.0, const("freq"), ALU.mult, ALU.mult).then_inc(emb_step, 1)
            dve.wait_ge(emb_step, 2)
            reduce_angle(emb_e[:, :], emb_t[:, :], const("turns"), const("phase"), emb_reduced).then_inc(emb_angle, 1)

            dve.wait_ge(emb_exp, 1)
            dve.tensor_scalar(emb_t[:, :], emb_t[:, :], 1.0, None, ALU.add).then_inc(emb_step, 1)
            dve.wait_ge(emb_step, 3)
            dve.reciprocal(emb_e[:, :], emb_t[:, :]).then_inc(emb_step, 1)
            dve.wait_ge(emb_step, 4)
            dve.tensor_tensor(emb_tok[:, :, :], emb_s[:, :].unsqueeze(2).to_broadcast([P, B, S]),
                              emb_e[:, :].unsqueeze(2).to_broadcast([P, B, S]), ALU.mult).then_inc(emb_set, 1)
            dve.wait_ge(rot_spread, 1)
            dve.tensor_copy(rot[:, :, :].rearrange("p t c -> p (t c)"), ps[0][:, 3, 0:NT * 9]).then_inc(rot_set, 1)

            dve.wait_ge(cols_in, 16)
            for layer in (1, 3):
                dve.tensor_scalar(qbias[:, layer // 2, :], const("qspread"), col(f"bq{layer}"), None,
                                  ALU.mult).then_inc(qbias_set, 1)

            def rotate(h):
                dve.wait_ge(x_in[h], 16)
                dve.wait_ge(rot_set, 1)
                t0 = h * TILES
                x4 = xin[h][:, :, :].rearrange("p t (i c) -> p t i c", c=4)
                sin_part = norm[h][:, :, :].rearrange("p t (i a c) -> p t i a c", a=2, c=2)
                x5 = xin[h][:, :, :].rearrange("p t (i a c) -> p t i a c", a=2, c=2)
                s4 = rot[:, t0:t0 + TILES, 4:8].rearrange("p t (a c) -> p t a c", c=2)
                for c in range(2):
                    dve.tensor_tensor(sin_part[:, :, :, :, c], x5[:, :, :, :, 1 - c],
                                      s4[:, :, :, c].unsqueeze(2).to_broadcast([P, TILES, D // 4, 2]),
                                      ALU.mult).then_inc(rotated[h], 1)
                dve.tensor_tensor(xrot[h][:, :, :].rearrange("p t (i c) -> p t i c", c=4), x4,
                                  rot[:, t0:t0 + TILES, 0:4].unsqueeze(2).to_broadcast([P, TILES, D // 4, 4]),
                                  ALU.mult).then_inc(rotated[h], 1)
                dve.wait_ge(rotated[h], 3)
                dve.tensor_tensor(xrot[h][:, :, :], xrot[h][:, :, :], norm[h][:, :, :], ALU.add).then_inc(rotated[h], 1)
                dve.wait_ge(rotated[h], 4)

            def norm_stats(n, h, src):
                for t in range(TILES):
                    dve.bn_stats(stats[h][:, t, :], src[h][:, t, :]).then_inc(stats_made[h], 1)
                for t in range(TILES):
                    dve.wait_ge(stats_made[h], upto_norm(n, t + 1, TILES))
                    dve.bn_aggr(mv[h][:, t, :], stats[h][:, t, :]).then_inc(stats_summed[h], 1)
                dve.wait_ge(stats_summed[h], upto_norm(n, TILES, TILES + 1))
                dve.tensor_scalar(rstd[h][:, :], mv[h][:, :, 1], EPS, None, ALU.add).then_inc(stats_summed[h], 1)

            def norm_apply(n, h, src):
                dve.wait_ge(scale_made[h], upto_norm(n, 1, 1))
                for t in range(TILES):
                    dve.tensor_scalar(norm[h][:, t, :], src[h][:, t, :], mv[h][:, t, 0:1], rstd[h][:, t:t + 1],
                                      ALU.subtract, ALU.mult).then_inc(normed[h], 1)

            def ada_copy(h):
                dve.wait_ge(ada_made[h], 1)
                dve.tensor_tensor(ada[h][:, :, :], ps[h][:, 0:2, :].rearrange("p c (t n) -> p (c t) n", t=2),
                                  rows_sb[:, 0:2, :].rearrange("p r n -> p (r n)").unsqueeze(1)
                                  .to_broadcast([P, TILES, 2 * D]), ALU.add).then_inc(ada_set[h], 1)

            def modulate(h):
                dve.wait_ge(ada_set[h], 1)
                dve.wait_ge(normed[h], upto_norm(0, TILES, TILES))
                dve.tensor_tensor(res[h][:, :, :], norm[h][:, :, :], ada[h][:, :, 0:D], ALU.mult).then_inc(modulated[h], 1)
                dve.wait_ge(modulated[h], 1)
                dve.tensor_tensor(res[h][:, :, :], res[h][:, :, :], ada[h][:, :, D:2 * D], ALU.add).then_inc(modulated[h], 1)

            def spread_k(layer, h):
                dve.wait_ge(k_made[h], upto(layer, 1, 1))
                for g in range(G):
                    dve.tensor_scalar(ks[h][:, :, g, :], ps[h][:, 1, :].rearrange("p (b s) -> p b s", b=HB),
                                      col(f"bk{layer}"), const("kspread")[:, g:g + 1], ALU.add,
                                      ALU.mult).then_inc(k_spread[h], 1)

            def spread_v(layer, h):
                dve.wait_ge(v_made[h], upto(layer, 1, 1))
                dve.wait_ge(vs_zeroed, h + 1)
                for j in (2, 3):
                    v_copy(dve.tensor_copy, h, j).then_inc(v_spread[h], 1)

            def softmax(layer, h, n):
                pr = PAIRS[n]
                view = pair(sc, h, pr).rearrange("p b g s -> p (b g) s")
                dve.wait_ge(scored[h], upto(layer, n + 1, 2))
                if layer == 1:
                    dve.wait_ge(bias_masked[h], 4)
                    addend = pair(bias, h, pr).rearrange("p b g s -> p (b g) s")
                else:
                    addend = const("causal").unsqueeze(1).to_broadcast([P, 8 * G, S])
                dve.tensor_tensor(view, ps[h][:, 2 * pr:2 * pr + 2, :].rearrange("p c (n s) -> p (c n) s", s=S),
                                  addend, ALU.add).then_inc(biased[h], 1)
                top = pair(peak, h, pr).rearrange("p b g -> p (b g)")
                dve.wait_ge(biased[h], upto(layer, n + 1, 2))
                dve.tensor_reduce(top, view, AX.X, ALU.max).then_inc(peaked[h], 1)
                dve.wait_ge(peaked[h], upto(layer, n + 1, 2))
                dve.tensor_tensor(view, view, top.unsqueeze(2).to_broadcast([P, 8 * G, S]),
                                  ALU.subtract).then_inc(shifted[h], 1)

            def transpose_probs(layer, h, n):
                pr = PAIRS[n]
                dve.wait_ge(exped[h], upto(layer, n + 1, 2))
                dve.transpose(pair(pt, h, pr).rearrange("p b g s -> p (b g s)"),
                              pair(sc, h, pr).rearrange("p b g s -> p (b g s)")).then_inc(prob_T[h], 1)

            def context(layer, h):
                dve.wait_ge(sum_made[h], upto(layer, 1, 1))
                dve.reciprocal(rsum[h][:, :], ps[h][:, 3, :]).then_inc(recip_made[h], 1)
                dve.wait_ge(recip_made[h], upto(layer, 1, 1))
                dve.wait_ge(ctx_made[h], upto(layer, 1, 1))
                dve.tensor_tensor(ctxT[h][:, :], ps[h][:, 2, :], rsum[h][:, :], ALU.mult).then_inc(ctx_ready[h], 1)

            def middle(layer, h):
                dve.wait_ge(attn_made[h], upto(layer, 1, 1))
                dve.wait_ge(res_b_ready[h], upto(layer, 1, 1))
                dve.tensor_tensor(mid[h][:, :, :], tiles(h, 0), res_b[h][:, :, :], ALU.add).then_inc(mid_ready[h], 1)
                dve.wait_ge(mid_ready[h], upto(layer, 1, 1))
                norm_stats(1 if layer == 1 else 4, h, mid)

            rows_ready = sem("rows_ready")
            dve.wait_ge(rows_in, 16)
            dve.tensor_scalar(row("ada_scale"), row("ada_scale"), 1.0, None, ALU.add).then_inc(rows_ready, 1)
            for h in range(HALVES):
                rotate(h)
                norm_stats(0, h, xrot)
            dve.wait_ge(rows_ready, 1)
            for h in range(HALVES):
                ada_copy(h)
            for h in range(HALVES):
                norm_apply(0, h, xrot)
                modulate(h)
            dve.wait_ge(bo_made, 1)
            dve.tensor_tensor(bo_all[:, 0, :], ps[0][:, 2, 0:D], row("bo1"), ALU.add).then_inc(bo_set, 1)

            dve.wait_ge(expert_in, 48)
            dve.tensor_copy(hot[:, 0, :], domain_sb[:, :]).then_inc(hot_set, 1)
            dve.wait_ge(hot_set, 1)
            dve.tensor_scalar(hot[:, 2, :], hot[:, 0, :], 0.0, float(E - 1), ALU.max, ALU.min).then_inc(hot_set, 1)
            dve.wait_ge(hot_set, 2)
            dve.tensor_scalar(hot[:, 1, :], hot[:, 2, :], const("expert_no", E + 1), None,
                              ALU.is_equal).then_inc(hot_set, 1)
            dve.tensor_tensor(hot[:, 3, :], hot[:, 0, :], hot[:, 2, :], ALU.is_equal).then_inc(hot_set, 1)
            dve.wait_ge(hot_set, 4)
            dve.scalar_tensor_tensor(hot[:, 4, :], hot[:, 1, :], const("row_e", E + 1), hot[:, 3, :],
                                     ALU.subtract, ALU.mult).then_inc(hot_set, 1)
            dve.wait_ge(hot_set, 5)
            dve.tensor_scalar(hot[:, 5, :], hot[:, 4, :], const("row_e", E + 1), None, ALU.add).then_inc(hot_set, 1)

            for layer in (1, 3):
                for h in range(HALVES):
                    spread_k(layer, h)
                    spread_v(layer, h)
                for h in range(HALVES):
                    softmax(layer, h, 0)
                    softmax(layer, h, 1)
                for h in range(HALVES):
                    transpose_probs(layer, h, 0)
                    transpose_probs(layer, h, 1)
                for h in range(HALVES):
                    context(layer, h)
                for h in range(HALVES):
                    middle(layer, h)
                for h in range(HALVES):
                    norm_apply(1 if layer == 1 else 4, h, mid)
                if layer == 1:
                    dve.wait_ge(bo_made, 2)
                    dve.tensor_tensor(bo_all[:, 1, :], ps[1][:, 2, 0:D], row("bo3"), ALU.add).then_inc(bo_set, 1)
                    dve.wait_ge(sel_made, 1)
                    dve.tensor_copy(wselT[:, :, :].rearrange("a b o -> a o b"),
                                    ps[1][0:A, 2:4, :].rearrange("a c (o b) -> a (c o) b", b=B)).then_inc(sel_set, 1)
                    dve.wait_ge(ebias_made, 1)
                    dve.tensor_copy(ebias[:, :], ps[0][0:A, 2, 256:256 + B]).then_inc(dve_setup, 1)
                if layer == 1:
                    for h in range(HALVES):
                        dve.wait_ge(ffn2_made[h], 1)
                        dve.wait_ge(mid_b_ready[h], 1)
                        dve.tensor_tensor(post[h][:, :, :], tiles(h, 0), mid_b[h][:, :, :],
                                          ALU.add).then_inc(post_ready[h], 1)
                    for h in range(HALVES):
                        dve.wait_ge(expert_made[h], 1)
                        dve.wait_ge(dve_setup, 2)
                        dve.tensor_tensor(hid2[h][:, :].rearrange("a (b s) -> a b s", b=HB),
                                          ps[h][0:A, 3, :].rearrange("a (b s) -> a b s", b=HB),
                                          ebias[:, h * HB:(h + 1) * HB].unsqueeze(2).to_broadcast([A, HB, S]),
                                          ALU.add).then_inc(expert_biased[h], 1)
                    for h in range(HALVES):
                        dve.wait_ge(up_made[h], 1)
                        dve.wait_ge(post_ready[h], 2)
                        dve.tensor_tensor(mid[h][:, :, :], tiles(h, 0), post_b[h][:, :, :],
                                          ALU.add).then_inc(adapted[h], 1)
                        dve.wait_ge(adapted[h], 1)
                        norm_stats(2, h, mid)
                    for h in range(HALVES):
                        norm_apply(2, h, mid)
                        dve.wait_ge(normed[h], upto_norm(2, TILES, TILES))
                        dve.tensor_tensor(norm[h][:, :, :], norm[h][:, :, :],
                                          row("ln_g").unsqueeze(1).to_broadcast([P, TILES, D]),
                                          ALU.mult).then_inc(res3_set[h], 1)
                        dve.wait_ge(res3_set[h], 1)
                        dve.tensor_tensor(res[h][:, :, :], norm[h][:, :, :],
                                          row("ln_b").unsqueeze(1).to_broadcast([P, TILES, D]),
                                          ALU.add).then_inc(res3_set[h], 1)
                        dve.wait_ge(res3_set[h], 2)
                        norm_stats(3, h, res)
                    for h in range(HALVES):
                        norm_apply(3, h, res)
            for h in range(HALVES):
                dve.wait_ge(ffn2_made[h], upto(3, 1, 1))
                dve.wait_ge(mid_b_ready[h], upto(3, 2, 1))
                dve.tensor_tensor(post_b[h][:, :, :], tiles(h, 0), mid_b[h][:, :, :], ALU.add).then_inc(post_ready[h], 1)
                dve.wait_ge(post_ready[h], upto(3, 1, 2))
                for t in range(TILES):
                    dve.scalar_tensor_tensor(post[h][:, t, :], post_b[h][:, t, :], rot[:, h * TILES + t, 8:9],
                                             res[h][:, t, :], ALU.mult, ALU.add).then_inc(gated[h], 1)


def kernel(**inputs):
    import concourse.bacc as bacc
    from concourse.bass_utils import run_bass_kernel_spmd as run

    a = {name: np.asarray(value) for name, value in inputs.items()}

    def layer(prefix):
        parts = [a[prefix + n] for n in ("Wq", "Wk", "Wv", "Wo", "W1")]
        w2 = a[prefix + "W2"].reshape(FC, P, D).transpose(1, 0, 2).reshape(P, FC * D)
        return np.concatenate(parts + [w2], axis=1)

    def column(name):
        v = a[name].reshape(-1, P if a[name].size >= P else a[name].size)
        return np.pad(v, ((0, 0), (0, P - v.shape[1]))).T

    l1, l2, l3 = "L1_cond_", "L2_cond_", "L3_cond_"
    column_names = [l1 + n for n in ("bq", "bk", "bv", "g2", "beta2", "b1")] + \
        [l3 + n for n in ("bq", "bk", "bv", "gamma1", "beta1", "gamma2", "beta2", "b1")] + [l2 + "down_b"]
    row_names = [l1 + "b_ada", l1 + "bo", l1 + "b2", l2 + "up_b", l2 + "ln_gamma", l2 + "ln_beta",
                 l3 + "bo", l3 + "b2"]
    per_tile = (HALVES * TILES, TB)
    arrays = {
        "x": a["x"].reshape(HALVES * TILES, P, D).transpose(1, 0, 2),
        "fside": a["fside_Bx16xSxS_0"].reshape(B, G, J, S, S).transpose(2, 3, 0, 1, 4).reshape(P, B, G, S),
        "mask": a["mask_Bx1xSxS_bk0"].reshape(B, S, S).transpose(1, 0, 2),
        "cols": np.concatenate([column(n) for n in column_names] + [a[l2 + "down_W"].T], axis=1),
        "rows": np.concatenate([a[n] for n in row_names]),
        "consts": shape_constants(),
        "w_ada": a[l1 + "W_ada"],
        "w1": layer(l1),
        "w3": layer(l3),
        "experts": np.concatenate([a[l2 + "expert_W"].reshape(E, A * A), a[l2 + "expert_b"],
                                   a[l2 + "domain_emb"]], axis=1),
        "up_wT": a[l2 + "up_W"].T,
        "scalars": np.stack([a[n].reshape(per_tile).T for n in ("condB_theta", "condB_phi", "condB_gatescore")],
                            axis=1),
        "steps": a["itok_B_34_63"],
        "domains": a["itok_B_0_15"],
    }
    arrays = {name: np.ascontiguousarray(v) for name, v in arrays.items()}
    nc = bacc.Bacc("TRN2", target_bir_lowering=False, num_devices=1)
    args = [nc.dram_tensor(f"in_{name}", v.shape, mybir.dt.from_np(v.dtype), kind="ExternalInput").ap()
            for name, v in arrays.items()]
    out = nc.dram_tensor("out", (B, S, D), F32, kind="ExternalOutput").ap()
    cond_seq(nc, *args, out)
    r = run(nc, [{f"in_{name}": v for name, v in arrays.items()}], core_ids=[0])
    return r.results[0]["out"]
```

```python
from contextlib import ExitStack

import numpy as np

import concourse.bass as bass
from concourse import mybir

F32 = mybir.dt.float32
BF16 = mybir.dt.bfloat16
I32 = mybir.dt.int32
U8 = mybir.dt.uint8
ALU = mybir.AluOpType
ACT = mybir.ActivationFunctionType
AX = mybir.AxisListType

B, S, D, F, H = 32, 32, 128, 512, 16
DH = D // H
P = 128
CHUNKS = 4
HB = B // CHUNKS
TOK = HB * S
TILES = TOK // P
TB = P // S
G = D // 32
J = 32 // DH
FC = F // P
A, E = 32, 16
EPS = 1e-5
MASKED = -1e30
MAGIC = 12582912.0
TWO_PI_HI = 6.28125
TWO_PI_LO = 2 * np.pi - TWO_PI_HI
PI_BELOW = 3.1415925
NSTAT = 6

LAYER_STEPS = ["transposes_in", "features_in", "project_qk", "residual_in", "spread_k", "spread_q", "scores",
               "softmax", "subtract", "project_v", "exps", "spread_v", "transpose_probs", "context",
               "recip", "normalise", "attn_out", "middle", "rstd_mid", "norm_mid", "residual_mid", "transposes_mid",
               "features_mid", "ffn_in", "gelu", "ffn_out", "after_ffn"]
ADAPTER_STEPS = ["adapter_transposes", "adapter_residual", "adapter_features", "adapter_down",
                 "adapter_gelu", "adapter_expert", "adapter_bias", "adapter_up", "adapter_out",
                 "adapter_rstd", "adapter_norm", "rstd_in3", "norm_in3"]
STEPS = [(name, 1) for name in ["rotate", "rstd_in1", "modulate", "scale_mask"] + LAYER_STEPS] \
    + [(name, 2) for name in ADAPTER_STEPS] + [(name, 3) for name in LAYER_STEPS]
TURNS = (
    "000001001000021110110021110220012100023021223132011120033321023312101332321022320033322310101122"
    "220101030231321330011200121330332201133201321021030111102230232311003230102323201320123001312331"
    "00320101222313212101220011003301222230033111033230133202113233232132230123323321132321332333"
)

COLS = {}
for _name, _width in [("bq1", 1), ("bk1", 1), ("bv1", 1), ("g1", 1), ("beta1", 1), ("b11", FC),
                      ("bq3", 1), ("bk3", 1), ("bv3", 1), ("gin3", 1), ("bin3", 1), ("g3", 1),
                      ("beta3", 1), ("b13", FC), ("down_b", 1), ("down_wT", A)]:
    _at = sum(w for _, w in COLS.values())
    COLS[_name] = (_at, _width)
NCOLS = sum(w for _, w in COLS.values())

ROWS = ["ada_scale", "ada_shift", "bo1", "b21", "up_b", "ln_g", "ln_b", "bo3", "b23"]

CONSTS = {}
for _name, _width in [("ident", P), ("qspread", J), ("kspread", G), ("ones_diag", 32), ("causal", S),
                      ("freq", 1), ("turns", 1), ("phase", 1), ("to_tokens", P), ("expert_no", 1),
                      ("row_e", 1)]:
    _at = sum(w for _, w in CONSTS.values())
    CONSTS[_name] = (_at, _width)
NCONSTS = sum(w for _, w in CONSTS.values())


def shape_constants():
    c = np.zeros((P, NCONSTS), np.float32)
    p = np.arange(P)

    def put(name, value):
        at, width = CONSTS[name]
        c[:, at:at + width] = value

    put("ident", np.eye(P))
    put("qspread", (p[:, None] % 32 // DH == np.arange(J)) * DH ** -0.5)
    put("kspread", p[:, None] // 32 == np.arange(G))
    put("ones_diag", p[:, None] // S == np.arange(32) // DH)
    put("causal", np.where(np.arange(S) <= p[:, None] % S, 0.0, MASKED))
    half = D // 2
    freqs = np.exp(np.arange(half, dtype=np.float32) * np.float32(-np.log(10000.0) / (half - 1)))
    put("freq", np.concatenate([freqs, freqs])[:, None])
    put("turns", np.where(p < half, 0.0, 0.25)[:, None])
    put("phase", np.where(p < half, 0.0, np.pi / 2)[:, None])
    put("to_tokens", np.where(p[:, None] < TB, p[:, None] == p // S, 0))
    put("expert_no", p[:, None])
    put("row_e", p[:, None] == E)
    return c


def cond_seq(nc, x, fside, mask, cols, rows, consts, w_ada, w1, w3, experts, up_wT, scalars, steps,
             domains, out):
    with ExitStack() as ctx:
        def sb(name, shape, dt=F32):
            return ctx.enter_context(nc.sbuf_tensor(name, shape, dt))

        def sem(name):
            return ctx.enter_context(nc.semaphore(name))

        cols_sb = sb("cols_sb", [P, NCOLS])
        rows_sb = sb("rows_sb", [P, len(ROWS), D])
        const_sb = sb("const_sb", [P, NCONSTS])
        wada_sb = sb("wada_sb", [P, 2 * D])
        w_sb = {1: sb("w1_sb", [P, 4 * D + 2 * F]), 3: sb("w3_sb", [P, 4 * D + 2 * F])}
        expert_sb = sb("expert_sb", [E + 1, A * A + 2 * A])
        up_sb = sb("up_sb", [A, D])
        scalar_sb = sb("scalar_sb", [TB, 3, B // TB])
        steps_sb = sb("steps_sb", [P, B], I32)
        domain_sb = sb("domain_sb", [E + 1, B], I32)
        mask_u8 = sb("mask_u8", [P, B, S], U8)

        def col(name):
            at, width = COLS[name]
            return cols_sb[:, at:at + width]

        def row(name):
            return rows_sb[:, ROWS.index(name), :]

        def const(name, rows_=P):
            at, width = CONSTS[name]
            return const_sb[0:rows_, at:at + width]

        ident = const("ident")
        wq, wk, wv, wo, wf1, wf2 = ({} for _ in range(6))
        for layer in (1, 3):
            w = w_sb[layer]
            wq[layer], wk[layer], wv[layer], wo[layer] = (w[:, i * D:(i + 1) * D] for i in range(4))
            wf1[layer] = w[:, 4 * D:4 * D + F]
            wf2[layer] = w[:, 4 * D + F:4 * D + 2 * F].rearrange("p (c n) -> p c n", c=FC)

        angle = sb("angle", [TB, B // TB, 8])
        turn = sb("turn", [TB, B // TB, 8])
        rot4 = sb("rot4", [TB, B // TB, 9])
        rot = sb("rot", [P, B // TB, 9])
        emb_e = sb("emb_e", [P, B])
        emb_t = sb("emb_t", [P, B])
        emb = sb("emb", [P, P])
        ada_seq = sb("ada_seq", [P, 2 * D])
        of_token = sb("of_token", [P, B, S])
        hot = sb("hot", [E + 1, 6, B])
        wselT = sb("wselT", [A, B, A])
        ebias = sb("ebias", [A, B])
        qbias = sb("qbias", [P, 2, J])
        bo_all = sb("bo_all", [P, 2, D])
        half_pow = sb("half_pow", [P, TILES])
        mask_b = sb("mask_b", [P, B, S], BF16)
        ident_b = sb("ident_b", [P, P], BF16)
        causal_b = sb("causal_b", [P, S], BF16)

        def each(name, shape, dt=F32):
            return [sb(f"{name}_{c}", shape, dt) for c in range(CHUNKS)]

        xin = each("xin", [P, TILES, D])
        xrot = each("xrot", [P, TILES, D])
        res = each("res", [P, TILES, D])
        res_b = each("res_b", [P, TILES, D])
        mid = each("mid", [P, TILES, D])
        mid_b = each("mid_b", [P, TILES, D])
        post = each("post", [P, TILES, D])
        post_b = each("post_b", [P, TILES, D])
        norm = each("norm", [P, TILES, D])
        stats = each("stats", [P, TILES, NSTAT])
        mv = each("mv", [P, TILES, 2])
        rstd = each("rstd", [P, TILES])
        feat = each("feat", [P, TOK])
        qs = each("qs", [P, HB, J, S])
        ks = each("ks", [P, G, HB, S])
        vs = each("vs", [P, HB, G, 32])
        bias = sb("bias", [P, B, G, S])
        sc = each("sc", [P, HB, G, S])
        peak = each("peak", [P, HB, G])
        pt = each("pt", [P, HB, G, S])
        rsum = each("rsum", [P, TOK])
        ctxT = each("ctxT", [P, TOK])
        act = [q[:, :, :, :].rearrange("p b j s -> p (b j s)").rearrange("p (c n) -> p c n", c=FC) for q in qs]
        hid = [t[0:A, :] for t in ctxT]
        hid2 = [t[0:A, :] for t in rsum]

        ps = [ctx.enter_context(nc.psum_tensor(f"ps_{c}", [P, 4 * TOK], F32)) for c in range(CHUNKS)]

        def slot(c, i, width=TOK):
            return ps[c][:, i * TOK:i * TOK + width]

        def slot_tiles(c, i):
            return slot(c, i).rearrange("p (t n) -> p t n", t=TILES)

        (consts_in, cols_in, ada_rows_in, rows_in, wada_in, small_in, steps_in, up_in, expert_in,
         mask_in, out_done) = (
            sem(n) for n in ("consts_in", "cols_in", "ada_rows_in", "rows_in", "wada_in", "small_in",
                             "steps_in", "up_in", "expert_in", "mask_in", "out_done"))
        w_in = {1: sem("w1_in"), 3: sem("w3_in")}
        x_in = [sem("x_in_0"), sem("x_in_rest")]
        bias_in = [sem(f"bias_in_{c}") for c in range(CHUNKS)]

        (pool_setup, angles_set, sin_set, rot_spread, rot_set, emb_angle, emb_silu, emb_set,
         dve_steps, hot_set, sel_made, sel_set, bo_made, bo_set, small_set, seq_made) = (
            sem(n) for n in ("pool_setup", "angles_set", "sin_set", "rot_spread", "rot_set", "emb_angle",
                             "emb_silu", "emb_set", "dve_steps", "hot_set", "sel_made",
                             "sel_set", "bo_made", "bo_set", "small_set", "seq_made"))

        def per_chunk(name):
            return [sem(f"{name}_{c}") for c in range(CHUNKS)]

        (mask_scaled, ada_made, modulated, transposed, feat_ready, stats_done, scale_made, normed, projected,
         k_spread, q_spread, v_spread, scored, softmax_steps, subtracted, exped, prob_T, ctx_made,
         recip_made, ctx_ready, tokens_made, mid_ready, res_b_ready, mid_b_ready, ffn1_made, ffn_act, post_ready,
         adapter_made, down_act, adapter_steps) = (
            per_chunk(n) for n in ("mask_scaled", "ada_made", "modulated", "transposed", "feat_ready", "stats_done",
                                   "scale_made", "normed", "projected", "k_spread", "q_spread", "v_spread", "scored",
                                   "softmax_steps", "subtracted", "exped", "prob_T", "ctx_made", "recip_made",
                                   "ctx_ready", "tokens_made", "mid_ready", "res_b_ready", "mid_b_ready",
                                   "ffn1_made", "ffn_act", "post_ready", "adapter_made", "down_act",
                                   "adapter_steps"))

        def upto(layer, count, each_layer):
            return (layer // 2) * each_layer + count

        TRANSPOSE = {"in1": 1, "mid1": 2, "adapter": 3, "in3": 4, "mid3": 5}
        PRODUCT = {"attn1": 1, "ffn1": 2, "up": 3, "attn3": 4, "ffn3": 5}
        NORM = {"in1": 0, "mid1": 1, "adapter": 2, "in3": 3, "mid3": 4}
        NORMED = {"mid1": 1, "in3": 2, "mid3": 3}
        MIDDLE = {"mid1": 1, "adapter": 2, "mid3": 3}
        STAT_STEPS = 2 * TILES + 1

        def rows_of(tensor, c, b0=0, b1=HB):
            return tensor[c][:, b0:b1].rearrange("p b g s -> p (b g) s")

        def score_rows(c, b0=0, b1=HB):
            return ps[c][:, b0 * P:b1 * P].rearrange("p (n s) -> p n s", s=S)

        def peaks(c, b0=0, b1=HB):
            return peak[c][:, b0:b1, :].rearrange("p b g -> p (b g)").unsqueeze(2)\
                .to_broadcast([P, (b1 - b0) * G, S])

        LAST = CHUNKS - 1
        experts_ps, ebias_ps = ps[LAST][0:A, 0:A * B], ps[LAST][A:2 * A, 0:B]
        seq_ps = slot(2, 0)
        rot_ps, bo1_ps, bo3_ps = slot(1, 2, B // TB * 9), slot(1, 3, D), slot(0, 1, D)

        BANK = HB // 2
        SOFTMAX_STEPS = {1: 5, 3: 4}

        def run_steps(parts):
            done = [0] * CHUNKS
            for c in map(int, TURNS):
                name, layer = STEPS[done[c]]
                done[c] += 1
                if name in parts:
                    parts[name](layer, c)

        block = ctx.enter_context(nc.Block())

        @block.sync
        def _(sp):
            sp.dma_start(scalar_sb[:, :, :], scalars).then_inc(small_in, 16)
            sp.dma_start(const_sb[:, :], consts).then_inc(consts_in, 16)
            sp.dma_start(steps_sb[:, :], steps.partition_broadcast(P)).then_inc(steps_in, 16)
            sp.dma_start(xin[0][:, :, :], x[:, 0:TILES, :]).then_inc(x_in[0], 16)
            sp.dma_start(wada_sb[:, :], w_ada).then_inc(wada_in, 16)
            sp.dma_start(rows_sb[:, 0:2, :], rows[0:2, :].partition_broadcast(P)).then_inc(ada_rows_in, 16)
            sp.dma_start(cols_sb[:, :], cols).then_inc(cols_in, 16)
            sp.dma_start(w_sb[1][:, :], w1).then_inc(w_in[1], 16)
            sp.dma_start(rows_sb[:, 2:, :], rows[2:, :].partition_broadcast(P)).then_inc(rows_in, 16)
            for c in range(1, CHUNKS):
                sp.dma_start(xin[c][:, :, :], x[:, c * TILES:(c + 1) * TILES, :]).then_inc(x_in[1], 16)
            for j in range(J):
                sp.dma_start(mask_u8[j * S:(j + 1) * S, :, :], mask).then_inc(mask_in, 16)
            for c in range(CHUNKS):
                b0, b1 = c * HB, (c + 1) * HB
                sp.dma_start(bias[:, b0:b1], fside[:, b0:b1]).then_inc(bias_in[c], 16)
            sp.dma_start(w_sb[3][:, :], w3).then_inc(w_in[3], 16)
            for c in range(CHUNKS):
                sp.wait_ge(post_ready[c], 2 + TILES)
                dst = out.rearrange("(u b) s d -> (b s) u d", b=TB)[:, c * TILES:(c + 1) * TILES, :]
                sp.dma_start(dst, post[c][:, :, :]).then_inc(out_done, 16)
            sp.wait_ge(out_done, 16 * CHUNKS)

        @block.gpsimd
        def _(pool):
            pool.memset(half_pow[:, :], -0.5).then_inc(pool_setup, 1)
            pool.memset(emb[:, B:P], 0.0).then_inc(pool_setup, 1)
            pool.wait_ge(consts_in, 16)
            pool.tensor_copy(of_token[:, :, :],
                             ident[:, 0:B].unsqueeze(2).to_broadcast([P, B, S])).then_inc(pool_setup, 1)

            def norm_scale(which, c):
                pool.wait_ge(stats_done[c], (NORM[which] + 1) * STAT_STEPS)
                pool.tensor_tensor(rstd[c][:, :], rstd[c][:, :], half_pow[:, :], ALU.pow).then_inc(scale_made[c], 1)

            def scale_mask(c):
                b0, b1 = c * HB, (c + 1) * HB
                pool.wait_ge(mask_in, 16 * J)
                pool.memset(vs[c][:, :, :, :], 0.0).then_inc(mask_scaled[c], 1)
                pool.tensor_scalar(mask_b[:, b0:b1, :], mask_u8[:, b0:b1, :], MASKED, None,
                                   ALU.mult).then_inc(mask_scaled[c], 1)

            def add_row(dst, src, what):
                return pool.tensor_tensor(dst, src, what.unsqueeze(1).to_broadcast([P, TILES, D]), ALU.add)

            def residual_in(layer, c):
                pool.wait_ge(bo_set, layer // 2 + 1)
                if layer == 1:
                    pool.wait_ge(modulated[c], 4 + 2 * TILES)
                else:
                    pool.wait_ge(adapter_steps[c], 1 + 2 * TILES)
                add_row(res_b[c][:, :, :], res[c][:, :, :], bo_all[:, layer // 2, :]).then_inc(res_b_ready[c], 1)

            def residual_mid(layer, c):
                pool.wait_ge(mid_ready[c], MIDDLE[f"mid{layer}"])
                pool.wait_ge(rows_in, 16)
                add_row(mid_b[c][:, :, :], mid[c][:, :, :], row(f"b2{layer}")).then_inc(mid_b_ready[c], 1)
                if layer == 3:
                    t0 = c * TILES
                    gate = rot[:, t0:t0 + TILES, 8:9].to_broadcast([P, TILES, D])
                    for n, (what, op) in enumerate([(res[c][:, :, :], ALU.subtract), (gate, ALU.mult),
                                                    (res[c][:, :, :], ALU.add)]):
                        pool.wait_ge(mid_b_ready[c], upto(3, n + 1, 1))
                        pool.tensor_tensor(mid_b[c][:, :, :], mid_b[c][:, :, :], what,
                                           op).then_inc(mid_b_ready[c], 1)

            def subtract(layer, c):
                if layer == 1:
                    pool.wait_ge(softmax_steps[c], 4)
                    pool.tensor_tensor(rows_of(sc, c, BANK), rows_of(sc, c, BANK), peaks(c, BANK),
                                       ALU.subtract).then_inc(subtracted[c], 1)

            def adapter_residual(c):
                pool.wait_ge(post_ready[c], 1)
                add_row(post_b[c][:, :, :], post[c][:, :, :], row("up_b")).then_inc(post_ready[c], 1)

            run_steps({
                "rstd_in1": lambda layer, c: norm_scale("in1", c), "scale_mask": lambda layer, c: scale_mask(c),
                "residual_in": residual_in, "subtract": subtract,
                "rstd_mid": lambda layer, c: norm_scale(f"mid{layer}", c), "residual_mid": residual_mid,
                "adapter_residual": lambda layer, c: adapter_residual(c),
                "adapter_rstd": lambda layer, c: norm_scale("adapter", c),
                "rstd_in3": lambda layer, c: norm_scale("in3", c)})

        @block.scalar
        def _(sca):
            sca.preload_act_table_set("silu_and_others")
            sca.wait_ge(angles_set, 1)
            sca.activation(rot4[:, :, 0:8], angle[:, :, :], ACT.Sin).then_inc(sin_set, 1)
            sca.wait_ge(emb_angle, 1)
            sca.activation(emb_t[:, :], emb_e[:, :], ACT.Sin).then_inc(sin_set, 1)
            sca.wait_ge(sin_set, 2)
            sca.activation(emb[:, 0:B], emb_t[:, :], ACT.Silu).then_inc(emb_silu, 1)
            sca.dma_start(domain_sb[:, :], domains.partition_broadcast(E + 1)).then_inc(expert_in, 16)
            sca.dma_start(expert_sb[0:E, :], experts).then_inc(expert_in, 16)
            at = CONSTS["ident"][0]
            sca.dma_start(expert_sb[E:E + 1, 0:A * A].rearrange("p (o a) -> p o a", o=A),
                          consts[0:A, at:at + A].unsqueeze(0)).then_inc(expert_in, 16)
            sca.dma_start(up_sb[:, :], up_wT).then_inc(up_in, 16)
            sca.preload_act_table_set("natural_log_exp_and_others")

            def take_experts():
                sca.wait_ge(sel_made, 1)
                sca.copy(wselT[:, :, :].rearrange("a b o -> a o b"),
                         experts_ps.rearrange("a (o b) -> a o b", b=B)).then_inc(sel_set, 1)
                sca.copy(ebias[:, :], ebias_ps).then_inc(sel_set, 1)

            def features(which, c, at_slot, affine=None):
                sca.wait_ge(transposed[c], TRANSPOSE[which])
                sca.wait_ge(cols_in, 16)
                if affine:
                    ins = sca.activation(feat[c][:, :], slot(c, at_slot), ACT.Identity, scale=col(affine[0]),
                                         bias=col(affine[1]))
                else:
                    ins = sca.activation(feat[c][:, :], slot(c, at_slot), ACT.Copy)
                ins.then_inc(feat_ready[c], 1)

            def features_in(layer, c):
                features(f"in{layer}", c, 3, ("gin3", "bin3") if layer == 3 else None)

            def features_mid(layer, c):
                features(f"mid{layer}", c, 0, (f"g{layer}", f"beta{layer}"))

            def spread_q(layer, c):
                sca.wait_ge(small_set, 2)
                sca.wait_ge(projected[c], upto(layer, 2, 3))
                for j in range(J):
                    sca.activation(qs[c][:, :, j, :], slot(c, 0).rearrange("p (b s) -> p b s", b=HB),
                                   ACT.Identity, scale=const("qspread")[:, j:j + 1],
                                   bias=qbias[:, layer // 2, j:j + 1]).then_inc(q_spread[c], 1)

            def spread_v(layer, c):
                sca.wait_ge(projected[c], upto(layer, 3, 3))
                sca.wait_ge(mask_scaled[c], 1)
                for j in range(J):
                    src = slot(c, 1)[j * 32:(j + 1) * 32, :].rearrange("p (n d) -> p n d", d=DH)
                    dst = vs[c][j * 32:(j + 1) * 32].rearrange("p b g f -> p (b g) f")
                    sca.copy(dst[:, :, j * DH:(j + 1) * DH], src).then_inc(v_spread[c], 1)

            def exps(layer, c):
                sca.wait_ge(softmax_steps[c], upto(layer, SOFTMAX_STEPS[layer], SOFTMAX_STEPS[1]))
                if layer == 1:
                    sca.wait_ge(subtracted[c], 1)
                sca.activation(rows_of(sc, c), rows_of(sc, c), ACT.Exp).then_inc(exped[c], 1)

            def recip(layer, c):
                sca.wait_ge(ctx_made[c], upto(layer, 1, 2))
                sca.activation(rsum[c][:, :], slot(c, 2), ACT.Ln).then_inc(recip_made[c], 1)
                sca.wait_ge(recip_made[c], upto(layer, 1, 2))
                sca.activation(rsum[c][:, :], rsum[c][:, :], ACT.Exp, scale=-1.0).then_inc(recip_made[c], 1)

            def gelu(layer, c):
                func = ACT.Gelu_apprx_sigmoid if layer == 1 else ACT.Gelu
                for i in range(FC):
                    sca.wait_ge(ffn1_made[c], upto(layer, 2 * (i // 2) + 2, FC))
                    sca.activation(act[c][:, i, :], slot(c, i), func,
                                   bias=col(f"b1{layer}")[:, i:i + 1]).then_inc(ffn_act[c], 1)

            def adapter_gelu(c):
                sca.wait_ge(adapter_made[c], 1)
                sca.activation(hid[c], slot(c, 0)[0:A, :], ACT.Gelu,
                               bias=col("down_b")[0:A, :]).then_inc(down_act[c], 1)

            run_steps({
                "rotate": lambda layer, c: take_experts() if c == LAST else None,
                "features_in": features_in, "spread_q": spread_q, "spread_v": spread_v, "exps": exps, "recip": recip,
                "features_mid": features_mid, "gelu": gelu,
                "adapter_features": lambda layer, c: features("adapter", c, 3),
                "adapter_gelu": lambda layer, c: adapter_gelu(c)})

        @block.tensor
        def _(pe):
            def transpose_tiles(src, c, at_slot, tile_ready=None):
                for t in range(TILES):
                    if tile_ready:
                        pe.wait_ge(tile_ready[0], tile_ready[1] + t)
                    last = pe.transpose(slot(c, at_slot)[:, t * P:(t + 1) * P], src[c][:, t, :], ident)
                last.then_inc(transposed[c], 1)

            pe.wait_ge(consts_in, 16)
            pe.wait_ge(sin_set, 1)
            pe.matmul(rot_ps, const("to_tokens", TB),
                      rot4[:, :, :].rearrange("p t c -> p (t c)"), start=True, stop=True).then_inc(rot_spread, 1)

            def choose_experts():
                pe.wait_ge(expert_in, 48)
                pe.wait_ge(hot_set, 1)
                for o in range(A):
                    pe.matmul(experts_ps[:, o * B:(o + 1) * B], expert_sb[:, o * A:(o + 1) * A],
                              hot[:, 5, :], start=True, stop=True)
                pe.matmul(ebias_ps, expert_sb[0:E, A * A:A * A + A], hot[0:E, 5, :], start=True,
                          stop=False)
                pe.matmul(ebias_ps, expert_sb[0:E, A * A + A:A * A + 2 * A], hot[0:E, 1, :],
                          start=False, stop=True).then_inc(sel_made, 1)

            pe.wait_ge(wada_in, 16)
            pe.wait_ge(emb_silu, 1)
            pe.wait_ge(pool_setup, 3)
            pe.matmul(seq_ps, emb[:, :], wada_sb[:, :], start=True, stop=True).then_inc(seq_made, 1)
            def bv_out(layer, where):
                pe.wait_ge(w_in[layer], 16)
                pe.matmul(where, col(f"bv{layer}").to_broadcast([P, P]), wo[layer], start=True,
                          stop=True).then_inc(bo_made, 1)

            def ada(c):
                pe.wait_ge(emb_set, 1)
                if c == LAST:
                    pe.wait_ge(sel_set, 2)
                for t in range(TILES):
                    b0 = c * HB + t * TB
                    last = pe.matmul(ps[c][:, t * 2 * D:(t + 1) * 2 * D],
                                     of_token[:, b0:b0 + TB, :].rearrange("p b s -> p (b s)"),
                                     ada_seq[:, :], start=True, stop=True)
                last.then_inc(ada_made[c], 1)
                if c == 0:
                    pe.wait_ge(cols_in, 16)
                    pe.wait_ge(rot_set, 1)
                    bv_out(1, bo1_ps)

            def transposes_in(layer, c):
                if layer == 1:
                    if c == 1:
                        pe.wait_ge(bo_set, 1)
                    transpose_tiles(res, c, 3, (modulated[c], 4 + TILES + 1))
                else:
                    transpose_tiles(norm, c, 3, (normed[c], (NORMED["in3"] - 1) * TILES + 1))

            def project_qk(layer, c):
                pe.wait_ge(feat_ready[c], TRANSPOSE[f"in{layer}"])
                for i, w in ((2, wk[layer]), (0, wq[layer])):
                    pe.matmul(slot(c, i), w, feat[c][:, :], start=True, stop=True).then_inc(projected[c], 1)

            def project_v(layer, c):
                pe.wait_ge(softmax_steps[c], 2 if layer == 1 else upto(3, SOFTMAX_STEPS[3], SOFTMAX_STEPS[1]))
                for b in range(HB):
                    for j in range(J):
                        last = pe.matmul(slot(c, 1)[j * 32:(j + 1) * 32, b * 32:(b + 1) * 32],
                                         feat[c][:, b * S:(b + 1) * S],
                                         wv[layer].rearrange("p (g f) -> p g f", g=G)[:, :, j * DH:(j + 1) * DH],
                                         start=True, stop=True)
                last.then_inc(projected[c], 1)

            def scores(layer, c):
                pe.wait_ge(small_set, 3)
                pe.wait_ge(k_spread[c], upto(layer, 1, 1))
                pe.wait_ge(q_spread[c], upto(layer, J, J))
                if layer == 1:
                    pe.wait_ge(mask_scaled[c], 2)
                for b in range(HB):
                    if b % 4 == 0:
                        if layer == 1:
                            b0 = c * HB + b
                            masks = mask_b[:, b0:b0 + 4, :].unsqueeze(2).to_broadcast([P, 4, G, S])
                        else:
                            masks = causal_b[:, :].unsqueeze(1).to_broadcast([P, 4 * G, S])
                        pe.matmul(ps[c][:, b * P:(b + 4) * P], ident_b[:, :], masks, start=True, stop=False)
                    last = pe.matmul(ps[c][:, b * P:(b + 1) * P], qs[c][:, b].rearrange("p j s -> p (j s)"),
                                     ks[c][:, :, b, :], start=False, stop=(b % 4 == 3))
                    if b % BANK == BANK - 1:
                        last.then_inc(scored[c], 1)

            def context(layer, c):
                pe.wait_ge(prob_T[c], upto(layer, 1, 1))
                pe.wait_ge(v_spread[c], upto(layer, J, J))
                for g in range(G):
                    last = pe.matmul(slot(c, 2)[32 * g:32 * g + 32, :], const("ones_diag"), pt[c][:, :, g, :],
                                     start=True, stop=True)
                last.then_inc(ctx_made[c], 1)
                for b in range(HB):
                    for g in range(G):
                        last = pe.matmul(slot(c, 0)[32 * g:32 * g + 32, b * S:(b + 1) * S],
                                         vs[c][:, b, g, :], pt[c][:, b, g, :], start=True, stop=True)
                last.then_inc(ctx_made[c], 1)

            def attn_out(layer, c):
                pe.wait_ge(ctx_ready[c], upto(layer, 1, 1))
                for t in range(TILES):
                    last = pe.matmul(slot(c, 3)[:, t * D:(t + 1) * D], ctxT[c][:, t * P:(t + 1) * P], wo[layer],
                                     start=True, stop=True)
                last.then_inc(tokens_made[c], 1)

            def transposes_mid(layer, c):
                transpose_tiles(norm, c, 0, (normed[c], (NORMED[f"mid{layer}"] - 1) * TILES + 1))

            def ffn_in(layer, c):
                pe.wait_ge(feat_ready[c], TRANSPOSE[f"mid{layer}"])
                for i in range(FC):
                    pe.matmul(slot(c, i), wf1[layer][:, i * P:(i + 1) * P], feat[c][:, :], start=True,
                              stop=True).then_inc(ffn1_made[c], 1)

            def ffn_out(layer, c):
                for t in range(TILES):
                    for i in range(FC):
                        if t == 0:
                            pe.wait_ge(ffn_act[c], upto(layer, max(i + 1, 2), FC))
                        last = pe.matmul(slot(c, 0)[:, t * D:(t + 1) * D], act[c][:, i, t * P:(t + 1) * P],
                                         wf2[layer][:, i, :], start=(i == 0), stop=(i == FC - 1))
                last.then_inc(tokens_made[c], 1)

            def adapter_transposes(c):
                pe.wait_ge(post_ready[c], 1)
                transpose_tiles(post, c, 3)
                if c == 0:
                    bv_out(3, bo3_ps)

            def adapter_down(c):
                pe.wait_ge(feat_ready[c], TRANSPOSE["adapter"])
                pe.matmul(slot(c, 0)[0:A, :], col("down_wT"), feat[c][:, :], start=True, stop=True)\
                    .then_inc(adapter_made[c], 1)

            def adapter_expert(c):
                pe.wait_ge(down_act[c], 1)
                for b in range(HB):
                    last = pe.matmul(slot(c, 2)[0:A, b * S:(b + 1) * S], wselT[:, c * HB + b, :],
                                     hid[c][:, b * S:(b + 1) * S], start=True, stop=True)
                last.then_inc(adapter_made[c], 1)

            def adapter_up(c):
                pe.wait_ge(adapter_steps[c], 1)
                pe.wait_ge(up_in, 16)
                for t in range(TILES):
                    last = pe.matmul(slot(c, 0)[:, t * D:(t + 1) * D], hid2[c][:, t * P:(t + 1) * P], up_sb[:, :],
                                     start=True, stop=True)
                last.then_inc(tokens_made[c], 1)

            run_steps({
                "rotate": lambda layer, c: choose_experts() if c == LAST else None,
                "rstd_in1": lambda layer, c: ada(c), "transposes_in": transposes_in, "project_qk": project_qk,
                "scores": scores, "project_v": project_v, "context": context,
                "attn_out": attn_out, "transposes_mid": transposes_mid, "ffn_in": ffn_in, "ffn_out": ffn_out,
                "adapter_transposes": lambda layer, c: adapter_transposes(c),
                "adapter_down": lambda layer, c: adapter_down(c),
                "adapter_expert": lambda layer, c: adapter_expert(c),
                "adapter_up": lambda layer, c: adapter_up(c)})

        @block.vector
        def _(dve):
            linked = [0]

            def link(ins):
                linked[0] += 1
                ins.then_inc(dve_steps, 1)
                dve.wait_ge(dve_steps, linked[0])

            def reduce_angle(a, t, turns, phase):
                link(dve.tensor_scalar(t, a, 1 / (2 * np.pi), turns, ALU.mult, ALU.add))
                link(dve.tensor_scalar(t, t, MAGIC, None, ALU.add))
                link(dve.tensor_scalar(t, t, -MAGIC, None, ALU.add))
                link(dve.scalar_tensor_tensor(a, t, -TWO_PI_HI, a, ALU.mult, ALU.add))
                link(dve.scalar_tensor_tensor(a, t, -float(TWO_PI_LO), a, ALU.mult, ALU.add))
                link(dve.tensor_scalar(a, a, phase, PI_BELOW, ALU.add, ALU.min))
                return dve.tensor_scalar(a, a, -PI_BELOW, None, ALU.max)

            dve.wait_ge(small_in, 16)
            link(dve.tensor_copy(rot4[:, :, 8], scalar_sb[:, 2, :]))
            for which in range(2):
                src = scalar_sb[:, which, :]
                for i in (0, 1):
                    dve.tensor_scalar(angle[:, :, 2 * which + i], src, float(np.pi / 2), None, ALU.add)
                dve.tensor_copy(angle[:, :, 4 + 2 * which], src)
                last = dve.tensor_scalar(angle[:, :, 5 + 2 * which], src, -1.0, None, ALU.mult)
            link(last)
            reduce_angle(angle[:, :, :], turn[:, :, :], 0.0, 0.0).then_inc(angles_set, 1)

            dve.wait_ge(consts_in, 16)
            dve.wait_ge(steps_in, 16)
            link(dve.tensor_copy(emb_t[:, :], steps_sb[:, :]))
            link(dve.tensor_scalar(emb_e[:, :], emb_t[:, :], 40.0, const("freq"), ALU.mult, ALU.mult))
            reduce_angle(emb_e[:, :], emb_t[:, :], const("turns"), const("phase")).then_inc(emb_angle, 1)

            dve.wait_ge(rot_spread, 1)
            dve.tensor_copy(rot[:, :, :].rearrange("p t c -> p (t c)"), rot_ps).then_inc(rot_set, 1)

            def one_hot_domains():
                dve.wait_ge(expert_in, 48)
                link(dve.tensor_copy(hot[:, 0, :], domain_sb[:, :]))
                link(dve.tensor_scalar(hot[:, 2, :], hot[:, 0, :], 0.0, float(E - 1), ALU.max, ALU.min))
                dve.tensor_tensor(hot[:, 3, :], hot[:, 0, :], hot[:, 2, :], ALU.is_equal)
                link(dve.tensor_scalar(hot[:, 1, :], hot[:, 2, :], const("expert_no", E + 1), None, ALU.is_equal))
                link(dve.scalar_tensor_tensor(hot[:, 4, :], hot[:, 1, :], const("row_e", E + 1), hot[:, 3, :],
                                              ALU.subtract, ALU.mult))
                dve.tensor_scalar(hot[:, 5, :], hot[:, 4, :], const("row_e", E + 1), None,
                                  ALU.add).then_inc(hot_set, 1)

            def small_operands():
                dve.wait_ge(cols_in, 16)
                for layer in (1, 3):
                    dve.tensor_scalar(qbias[:, layer // 2, :], const("qspread"), col(f"bq{layer}"), None,
                                      ALU.mult).then_inc(small_set, 1)
                dve.tensor_copy(causal_b[:, :], const("causal"))
                dve.tensor_copy(ident_b[:, :], ident).then_inc(small_set, 1)

            def norm_stats(which, c, src, tile_ready=None):
                n = NORM[which] * STAT_STEPS
                for t in range(TILES):
                    if tile_ready:
                        dve.wait_ge(tile_ready[0], tile_ready[1] + t)
                    dve.bn_stats(stats[c][:, t, :], src[c][:, t, :]).then_inc(stats_done[c], 1)
                for t in range(TILES):
                    dve.wait_ge(stats_done[c], n + t + 1)
                    dve.bn_aggr(mv[c][:, t, :], stats[c][:, t, :]).then_inc(stats_done[c], 1)
                dve.wait_ge(stats_done[c], n + 2 * TILES)
                dve.tensor_scalar(rstd[c][:, :], mv[c][:, :, 1], EPS, None, ALU.add).then_inc(stats_done[c], 1)

            def norm_apply(which, c, src):
                dve.wait_ge(scale_made[c], NORM[which] + 1)
                for t in range(TILES):
                    dve.tensor_scalar(norm[c][:, t, :], src[c][:, t, :], mv[c][:, t, 0:1], rstd[c][:, t:t + 1],
                                      ALU.subtract, ALU.mult).then_inc(normed[c], 1)

            def rotate(c):
                dve.wait_ge(x_in[min(c, 1)], 16 if c == 0 else 16 * (CHUNKS - 1))
                dve.wait_ge(rot_set, 1)
                t0 = c * TILES
                x4 = xin[c][:, :, :].rearrange("p t (i f) -> p t i f", f=4)
                x5 = xin[c][:, :, :].rearrange("p t (i a f) -> p t i a f", a=2, f=2)
                sin_part = norm[c][:, :, :].rearrange("p t (i a f) -> p t i a f", a=2, f=2)
                s4 = rot[:, t0:t0 + TILES, 4:8].rearrange("p t (a f) -> p t a f", f=2)
                for i in range(2):
                    dve.tensor_tensor(sin_part[:, :, :, :, i], x5[:, :, :, :, 1 - i],
                                      s4[:, :, :, i].unsqueeze(2).to_broadcast([P, TILES, D // 4, 2]),
                                      ALU.mult).then_inc(modulated[c], 1)
                dve.tensor_tensor(xrot[c][:, :, :].rearrange("p t (i f) -> p t i f", f=4), x4,
                                  rot[:, t0:t0 + TILES, 0:4].unsqueeze(2).to_broadcast([P, TILES, D // 4, 4]),
                                  ALU.mult).then_inc(modulated[c], 1)
                if c == 0:
                    dve.wait_ge(ada_rows_in, 16)
                    link(dve.tensor_scalar(row("ada_scale"), row("ada_scale"), 1.0, None, ALU.add))
                    dve.wait_ge(seq_made, 1)
                    dve.tensor_tensor(ada_seq[:, :], seq_ps, rows_sb[:, 0:2, :].rearrange("p r n -> p (r n)"),
                                      ALU.add).then_inc(emb_set, 1)
                dve.wait_ge(modulated[c], 3)
                dve.tensor_tensor(xrot[c][:, :, :], xrot[c][:, :, :], norm[c][:, :, :],
                                  ALU.add).then_inc(modulated[c], 1)
                dve.wait_ge(modulated[c], 4)
                norm_stats("in1", c, xrot)
                if c == 0:
                    small_operands()
                elif c == 1:
                    one_hot_domains()

            def modulate(c):
                dve.wait_ge(ada_made[c], 1)
                dve.wait_ge(scale_made[c], NORM["in1"] + 1)
                ada = ps[c][:, 0:2 * TOK].rearrange("p (t r n) -> p t r n", t=TILES, r=2)
                for t in range(TILES):
                    dve.scalar_tensor_tensor(norm[c][:, t, :], xrot[c][:, t, :], mv[c][:, t, 0:1],
                                             ada[:, t, 0, :], ALU.subtract, ALU.mult).then_inc(modulated[c], 1)
                for t in range(TILES):
                    dve.wait_ge(modulated[c], 4 + t + 1)
                    dve.scalar_tensor_tensor(res[c][:, t, :], norm[c][:, t, :], rstd[c][:, t:t + 1],
                                             ada[:, t, 1, :], ALU.mult, ALU.add).then_inc(modulated[c], 1)
                if c == 0:
                    dve.wait_ge(bo_made, 1)
                    dve.wait_ge(rows_in, 16)
                    dve.tensor_tensor(bo_all[:, 0, :], bo1_ps, row("bo1"), ALU.add).then_inc(bo_set, 1)

            def spread_k(layer, c):
                dve.wait_ge(projected[c], upto(layer, 1, 3))
                dve.scalar_tensor_tensor(ks[c][:, :, :, :].rearrange("p g b s -> p g (b s)"),
                                         slot(c, 2).unsqueeze(1).to_broadcast([P, G, TOK]), col(f"bk{layer}"),
                                         const("kspread").unsqueeze(2).to_broadcast([P, G, TOK]), ALU.add,
                                         ALU.mult).then_inc(k_spread[c], 1)

            def softmax(layer, c):
                banks = [(0, BANK), (BANK, HB)]
                src = [score_rows(c, *bank) for bank in banks]
                dst = [rows_of(sc, c, *bank) for bank in banks]
                if layer == 1:
                    dve.wait_ge(bias_in[c], 16)
                    for i, (b0, b1) in enumerate(banks):
                        dve.wait_ge(scored[c], i + 1)
                        dve.tensor_tensor(dst[i], src[i],
                                          bias[:, c * HB + b0:c * HB + b1].rearrange("p b g s -> p (b g) s"),
                                          ALU.add).then_inc(softmax_steps[c], 1)
                for i, (b0, b1) in enumerate(banks):
                    if layer == 1:
                        dve.wait_ge(softmax_steps[c], i + 1)
                    else:
                        dve.wait_ge(scored[c], upto(3, i + 1, 2))
                    dve.tensor_reduce(peak[c][:, b0:b1, :].rearrange("p b g -> p (b g)"),
                                      dst[i] if layer == 1 else src[i], AX.X, ALU.max).then_inc(softmax_steps[c], 1)
                if layer == 1:
                    dve.wait_ge(softmax_steps[c], 3)
                    dve.tensor_tensor(dst[0], dst[0], peaks(c, *banks[0]), ALU.subtract).then_inc(softmax_steps[c], 1)
                else:
                    for i, bank in enumerate(banks):
                        dve.wait_ge(softmax_steps[c], upto(3, i + 1, SOFTMAX_STEPS[1]))
                        dve.tensor_tensor(dst[i], src[i], peaks(c, *bank), ALU.subtract).then_inc(softmax_steps[c], 1)

            def transpose_probs(layer, c):
                dve.wait_ge(exped[c], upto(layer, 1, 1))
                dve.transpose(pt[c][:, :, :, :].rearrange("p b g s -> p (b g s)"),
                              sc[c][:, :, :, :].rearrange("p b g s -> p (b g s)")).then_inc(prob_T[c], 1)

            def normalise(layer, c):
                dve.wait_ge(ctx_made[c], upto(layer, 2, 2))
                dve.wait_ge(recip_made[c], upto(layer, 2, 2))
                dve.tensor_tensor(ctxT[c][:, :], slot(c, 0), rsum[c][:, :], ALU.mult).then_inc(ctx_ready[c], 1)

            def middle(layer, c):
                dve.wait_ge(tokens_made[c], PRODUCT[f"attn{layer}"])
                dve.wait_ge(res_b_ready[c], upto(layer, 1, 1))
                dve.tensor_tensor(mid[c][:, :, :], slot_tiles(c, 3), res_b[c][:, :, :],
                                  ALU.add).then_inc(mid_ready[c], 1)
                dve.wait_ge(mid_ready[c], MIDDLE[f"mid{layer}"])
                norm_stats(f"mid{layer}", c, mid)

            def norm_mid(layer, c):
                norm_apply(f"mid{layer}", c, mid)

            def after_ffn(layer, c):
                dve.wait_ge(tokens_made[c], PRODUCT[f"ffn{layer}"])
                if layer == 1:
                    dve.wait_ge(mid_b_ready[c], 1)
                    dve.tensor_tensor(post[c][:, :, :], slot_tiles(c, 0), mid_b[c][:, :, :],
                                      ALU.add).then_inc(post_ready[c], 1)
                else:
                    dve.wait_ge(mid_b_ready[c], upto(3, 4, 1))
                    for t in range(TILES):
                        dve.scalar_tensor_tensor(post[c][:, t, :], slot_tiles(c, 0)[:, t, :],
                                                 rot[:, c * TILES + t, 8:9], mid_b[c][:, t, :], ALU.mult,
                                                 ALU.add).then_inc(post_ready[c], 1)

            def adapter_bias(c):
                dve.wait_ge(adapter_made[c], 2)
                if c == 0:
                    dve.wait_ge(bo_made, 2)
                    dve.tensor_tensor(bo_all[:, 1, :], bo3_ps, row("bo3"), ALU.add).then_inc(bo_set, 1)
                dve.tensor_tensor(hid2[c].rearrange("a (b s) -> a b s", b=HB),
                                  slot(c, 2)[0:A, :].rearrange("a (b s) -> a b s", b=HB),
                                  ebias[:, c * HB:(c + 1) * HB].unsqueeze(2).to_broadcast([A, HB, S]),
                                  ALU.add).then_inc(adapter_steps[c], 1)

            def adapter_out(c):
                dve.wait_ge(tokens_made[c], PRODUCT["up"])
                dve.wait_ge(post_ready[c], 2)
                dve.tensor_tensor(mid[c][:, :, :], slot_tiles(c, 0), post_b[c][:, :, :],
                                  ALU.add).then_inc(mid_ready[c], 1)
                dve.wait_ge(mid_ready[c], MIDDLE["adapter"])
                norm_stats("adapter", c, mid)

            def adapter_norm(c):
                dve.wait_ge(scale_made[c], NORM["adapter"] + 1)
                for t in range(TILES):
                    dve.scalar_tensor_tensor(norm[c][:, t, :], mid[c][:, t, :], mv[c][:, t, 0:1], row("ln_g"),
                                             ALU.subtract, ALU.mult).then_inc(adapter_steps[c], 1)
                for t in range(TILES):
                    dve.wait_ge(adapter_steps[c], 1 + t + 1)
                    dve.scalar_tensor_tensor(res[c][:, t, :], norm[c][:, t, :], rstd[c][:, t:t + 1],
                                             row("ln_b"), ALU.mult, ALU.add).then_inc(adapter_steps[c], 1)
                norm_stats("in3", c, res, (adapter_steps[c], 1 + TILES + 1))

            def norm_in3(c):
                norm_apply("in3", c, res)

            run_steps({
                "rotate": lambda layer, c: rotate(c), "modulate": lambda layer, c: modulate(c),
                "spread_k": spread_k, "softmax": softmax, "transpose_probs": transpose_probs,
                "normalise": normalise, "middle": middle, "norm_mid": norm_mid, "after_ffn": after_ffn,
                "adapter_bias": lambda layer, c: adapter_bias(c), "adapter_out": lambda layer, c: adapter_out(c),
                "adapter_norm": lambda layer, c: adapter_norm(c), "norm_in3": lambda layer, c: norm_in3(c)})


def kernel(**inputs):
    import concourse.bacc as bacc
    from concourse.bass_utils import run_bass_kernel_spmd as run

    a = {name: np.asarray(value) for name, value in inputs.items()}

    def layer(prefix):
        parts = [a[prefix + n] for n in ("Wq", "Wk", "Wv", "Wo", "W1")]
        w2 = a[prefix + "W2"].reshape(FC, P, D).transpose(1, 0, 2).reshape(P, FC * D)
        return np.concatenate(parts + [w2], axis=1)

    def column(name):
        v = a[name].reshape(-1, P if a[name].size >= P else a[name].size)
        return np.pad(v, ((0, 0), (0, P - v.shape[1]))).T

    l1, l2, l3 = "L1_cond_", "L2_cond_", "L3_cond_"
    column_names = [l1 + n for n in ("bq", "bk", "bv", "g2", "beta2", "b1")] + \
        [l3 + n for n in ("bq", "bk", "bv", "gamma1", "beta1", "gamma2", "beta2", "b1")] + [l2 + "down_b"]
    row_names = [l1 + "b_ada", l1 + "bo", l1 + "b2", l2 + "up_b", l2 + "ln_gamma", l2 + "ln_beta",
                 l3 + "bo", l3 + "b2"]
    per_tile = (B // TB, TB)
    arrays = {
        "x": a["x"].reshape(B // TB, P, D).transpose(1, 0, 2),
        "fside": a["fside_Bx16xSxS_0"].reshape(B, G, J, S, S).transpose(2, 3, 0, 1, 4).reshape(P, B, G, S),
        "mask": a["mask_Bx1xSxS_bk0"].reshape(B, S, S).transpose(1, 0, 2),
        "cols": np.concatenate([column(n) for n in column_names] + [a[l2 + "down_W"].T], axis=1),
        "rows": np.concatenate([a[n] for n in row_names]).reshape(len(ROWS), D),
        "consts": shape_constants(),
        "w_ada": a[l1 + "W_ada"],
        "w1": layer(l1),
        "w3": layer(l3),
        "experts": np.concatenate([a[l2 + "expert_W"].reshape(E, A * A), a[l2 + "expert_b"],
                                   a[l2 + "domain_emb"]], axis=1),
        "up_wT": a[l2 + "up_W"].T,
        "scalars": np.stack([a[n].reshape(per_tile).T for n in ("condB_theta", "condB_phi", "condB_gatescore")],
                            axis=1),
        "steps": a["itok_B_34_63"],
        "domains": a["itok_B_0_15"],
    }
    arrays = {name: np.ascontiguousarray(v) for name, v in arrays.items()}
    nc = bacc.Bacc("TRN2", target_bir_lowering=False, num_devices=1)
    args = [nc.dram_tensor(f"in_{name}", v.shape, mybir.dt.from_np(v.dtype), kind="ExternalInput").ap()
            for name, v in arrays.items()]
    out = nc.dram_tensor("out", (B, S, D), F32, kind="ExternalOutput").ap()
    cond_seq(nc, *args, out)
    r = run(nc, [{f"in_{name}": v for name, v in arrays.items()}], core_ids=[0])
    return r.results[0]["out"]
```
